# Optimizing a Trainium2 kernel written in Bass

```python
import numpy as np
import jax
import jax.numpy as jnp

def _softmax(x, axis=-1):
    return jax.nn.softmax(x, axis=axis)

def _gelu(x):
    return jax.nn.gelu(x, approximate=True)

def _silu(x):
    return jax.nn.silu(x)

def _sigmoid(x):
    return jax.nn.sigmoid(x)

def _layernorm(x, axis=-1, eps=1e-05):
    m = jnp.mean(x, axis=axis, keepdims=True)
    v = jnp.var(x, axis=axis, keepdims=True)
    return (x - m) / jnp.sqrt(v + eps)

def _scatter_add(tgt, idx, src, axis=0):
    return tgt.at[idx].add(src)

def _segment_sum(src, seg, n):
    return jax.ops.segment_sum(src, seg, n)
kernel_name = 'mk_adaln_d1_jaxref_r8_4e1b55'

def setup_inputs(seed: int=0):
    np.random.seed(seed)
    _w = jnp.asarray

    def _L0_attn_setup():
        import jax, jax.numpy as jnp
        import numpy as np
        H, KV, HD, HID = (32, 8, 128, 512)
        THETA, FACTOR, HI_FF, LO_FF, ORIG_MAX = (500000.0, 8.0, 4.0, 1.0, 1024)

        def _llama3_inv_freq():
            inv = 1.0 / THETA ** (np.arange(0, HD, 2, dtype=np.float64) / HD)
            wavelen = 2.0 * np.pi / inv
            low_wl = ORIG_MAX / LO_FF
            high_wl = ORIG_MAX / HI_FF
            smooth = (ORIG_MAX / wavelen - LO_FF) / (HI_FF - LO_FF)
            scaled = np.where(wavelen > low_wl, inv / FACTOR, inv)
            mid = (wavelen <= low_wl) & (wavelen >= high_wl)
            scaled = np.where(mid, (1 - smooth) * inv / FACTOR + smooth * inv, scaled)
            return scaled.astype(np.float32)

        def _rope_cos_sin(T):
            inv = _llama3_inv_freq()
            pos = np.arange(T, dtype=np.float32)
            freqs = pos[:, None] * inv[None, :]
            emb = np.concatenate([freqs, freqs], axis=-1)
            return (jnp.asarray(np.cos(emb)), jnp.asarray(np.sin(emb)))

        def _rotate_half(x):
            x1, x2 = jnp.split(x, 2, axis=-1)
            return jnp.concatenate([-x2, x1], axis=-1)
        key = jax.random.key(seed)
        ks = jax.random.split(key, 5)
        s = 1.0 / np.sqrt(HID)
        return {'x': jax.random.normal(ks[0], (1, 256, HID), jnp.float32), 'wq': jax.random.normal(ks[1], (HID, H * HD), jnp.float32) * s, 'wk': jax.random.normal(ks[2], (HID, KV * HD), jnp.float32) * s, 'wv': jax.random.normal(ks[3], (HID, KV * HD), jnp.float32) * s, 'wo': jax.random.normal(ks[4], (H * HD, HID), jnp.float32) * s}
    _L0_attn_in = _L0_attn_setup()

    def _L0_ffn_setup():
        import jax, jax.numpy as jnp
        import numpy as np
        RANKS = (8, 16, 32, 64)
        TOPK = 1
        SCALING = 1.0 / 4
        key = jax.random.key(seed)
        ks = jax.random.split(key, 7)
        D_IN, D_OUT, MAX_R, N_RANKS = (512, 512, 64, len(RANKS))
        B_, S_ = (4, 256)
        return {'hidden_states': jax.random.normal(ks[0], (B_, S_, D_IN), jnp.float32), 'W': jax.random.normal(ks[1], (D_OUT, D_IN), jnp.float32) * 0.02, 'b': jax.random.normal(ks[2], (D_OUT,), jnp.float32) * 0.02, 'A': jax.random.normal(ks[3], (MAX_R, D_IN), jnp.float32) * 0.02, 'B': jnp.zeros((D_OUT, MAX_R), jnp.float32) + jax.random.normal(ks[4], (D_OUT, MAX_R), jnp.float32) * 0.02, 'gate_w': jax.random.normal(ks[5], (N_RANKS, D_IN), jnp.float32) * 0.02, 'gate_b': jax.random.normal(ks[6], (N_RANKS,), jnp.float32) * 0.02}
    _L0_ffn_in = _L0_ffn_setup()
    _L0_c = _w((lambda *s: np.random.randn(*s).astype(np.float32) * 0.05)(1, 512))
    _L0_wmod = _w((lambda *s: np.random.randn(*s).astype(np.float32) * 0.05)(512, 6 * 512) * 512 ** (-0.5))
    _d = {'L0_attn_x': _L0_attn_in['x'], 'L0_attn_wq': _L0_attn_in['wq'], 'L0_attn_wk': _L0_attn_in['wk'], 'L0_attn_wv': _L0_attn_in['wv'], 'L0_attn_wo': _L0_attn_in['wo'], 'L0_ffn_W': _L0_ffn_in['W'], 'L0_ffn_b': _L0_ffn_in['b'], 'L0_ffn_A': _L0_ffn_in['A'], 'L0_ffn_B': _L0_ffn_in['B'], 'L0_ffn_gate_w': _L0_ffn_in['gate_w'], 'L0_ffn_gate_b': _L0_ffn_in['gate_b'], 'L0_c': _L0_c, 'L0_wmod': _L0_wmod}
    _x0 = _d['L0_attn_x']
    _d['L0_attn_x'] = jax.random.normal(jax.random.fold_in(jax.random.key(seed), 1), (1, 1024, 512), dtype=_x0.dtype)
    del _x0
    return _d

def reference(L0_attn_x, L0_attn_wq, L0_attn_wk, L0_attn_wv, L0_attn_wo, L0_ffn_W, L0_ffn_b, L0_ffn_A, L0_ffn_B, L0_ffn_gate_w, L0_ffn_gate_b, L0_c, L0_wmod):

    def _L0_attn_ref(x, wq, wk, wv, wo):
        import jax, jax.numpy as jnp
        import numpy as np
        H, KV, HD, HID = (32, 8, 128, 512)
        THETA, FACTOR, HI_FF, LO_FF, ORIG_MAX = (500000.0, 8.0, 4.0, 1.0, 1024)

        def _llama3_inv_freq():
            inv = 1.0 / THETA ** (np.arange(0, HD, 2, dtype=np.float64) / HD)
            wavelen = 2.0 * np.pi / inv
            low_wl = ORIG_MAX / LO_FF
            high_wl = ORIG_MAX / HI_FF
            smooth = (ORIG_MAX / wavelen - LO_FF) / (HI_FF - LO_FF)
            scaled = np.where(wavelen > low_wl, inv / FACTOR, inv)
            mid = (wavelen <= low_wl) & (wavelen >= high_wl)
            scaled = np.where(mid, (1 - smooth) * inv / FACTOR + smooth * inv, scaled)
            return scaled.astype(np.float32)

        def _rope_cos_sin(T):
            inv = _llama3_inv_freq()
            pos = np.arange(T, dtype=np.float32)
            freqs = pos[:, None] * inv[None, :]
            emb = np.concatenate([freqs, freqs], axis=-1)
            return (jnp.asarray(np.cos(emb)), jnp.asarray(np.sin(emb)))

        def _rotate_half(x):
            x1, x2 = jnp.split(x, 2, axis=-1)
            return jnp.concatenate([-x2, x1], axis=-1)
        B, T, _ = x.shape
        q = (x @ wq).reshape(B, T, H, HD).transpose(0, 2, 1, 3)
        k = (x @ wk).reshape(B, T, KV, HD).transpose(0, 2, 1, 3)
        v = (x @ wv).reshape(B, T, KV, HD).transpose(0, 2, 1, 3)
        cos, sin = _rope_cos_sin(T)
        q = q * cos + _rotate_half(q) * sin
        k = k * cos + _rotate_half(k) * sin
        rep = H // KV
        k = jnp.repeat(k, rep, axis=1)
        v = jnp.repeat(v, rep, axis=1)
        scores = jnp.einsum('bhtd,bhsd->bhts', q, k) * (1.0 / np.sqrt(HD))
        mask = jnp.tril(jnp.ones((T, T), dtype=bool))
        scores = jnp.where(mask, scores, -jnp.inf)
        att = jax.nn.softmax(scores, axis=-1)
        out = jnp.einsum('bhts,bhsd->bhtd', att, v)
        out = out.transpose(0, 2, 1, 3).reshape(B, T, H * HD)
        return out @ wo

    def _L0_ffn_ref(hidden_states, W, b, A, B, gate_w, gate_b):
        import jax, jax.numpy as jnp
        import numpy as np
        RANKS = (8, 16, 32, 64)
        TOPK = 1
        SCALING = 1.0 / 4
        bsz, seq, d_in = hidden_states.shape
        out = jnp.einsum('bsd,od->bso', hidden_states, W) + b
        x = hidden_states.reshape(-1, d_in)
        scores = x @ gate_w.T + gate_b
        probs = jax.nn.softmax(scores, axis=-1)
        routing_weights, selected = jax.lax.top_k(probs, TOPK)
        routing_weights = routing_weights / jnp.sum(routing_weights, axis=-1, keepdims=True)
        lora_outputs = jnp.stack([x @ A[:r, :].T @ B[:, :r].T for r in RANKS], axis=1)
        sel = jnp.take_along_axis(lora_outputs, selected[:, :, None], axis=1)
        final = jnp.sum(sel * routing_weights[:, :, None], axis=1)
        return out + final.reshape(bsz, seq, -1)
    x = L0_attn_x
    mod = (_silu(L0_c) @ L0_wmod).reshape(L0_c.shape[0], 6, 1, -1)
    sa, ca, ga, sb, cb, gb = (mod[:, 0], mod[:, 1], mod[:, 2], mod[:, 3], mod[:, 4], mod[:, 5])
    ga = (2 * (ga >= 0) - 1) * jnp.maximum(jnp.abs(ga), 0.25)
    gb = (2 * (gb >= 0) - 1) * jnp.maximum(jnp.abs(gb), 0.25)
    h = _layernorm(x, axis=-1) * (1 + ca) + sa
    x = x + ga * _L0_attn_ref(h, L0_attn_wq, L0_attn_wk, L0_attn_wv, L0_attn_wo)
    h = _layernorm(x, axis=-1) * (1 + cb) + sb
    x = x + gb * _L0_ffn_ref(h, L0_ffn_W, L0_ffn_b, L0_ffn_A, L0_ffn_B, L0_ffn_gate_w, L0_ffn_gate_b)
    return x

_drawn_inputs = setup_inputs


def setup_inputs(seed=0):
    import zlib

    import numpy as np

    out = dict(_drawn_inputs(seed))
    spreads = {}
    factors = {'L0_ffn_b': 8.0,
     'L0_ffn_A': 4.572,
     'L0_ffn_B': 4.578,
     'L0_ffn_gate_w': 7.443,
     'L0_ffn_gate_b': 8.0}
    for name, (base, spread) in spreads.items():
        noise = np.random.default_rng([zlib.crc32(name.encode()), seed]).standard_normal(out[name].shape)
        drawn = base * np.exp(spread * noise) if base else spread * noise
        out[name] = jnp.asarray(drawn.astype(out[name].dtype))
    for name, factor in factors.items():
        out[name] = (out[name] * factor).astype(out[name].dtype)
    return out
```

```python
from contextlib import ExitStack

import numpy as np

import concourse.bass as bass
from concourse import mybir
from concourse.alu_op_type import AluOpType as ALU

ACT = mybir.ActivationFunctionType
AX_X = mybir.AxisListType.X
F32 = mybir.dt.float32
F32R = mybir.dt.float32r

P = 128
T = 1024
NT = T // P
D = 512
KC = D // P
HEADS, KV_HEADS, HD = 32, 8, 128
GROUPS = KV_HEADS
R = HEADS // KV_HEADS
HALF = 512
SCALE = 1.0 / float(np.sqrt(HD))
EPS = 1e-5
MASKED = -3.0e38
RANKS = (8, 16, 32, 64)
NR = len(RANKS)
MAX_R = RANKS[-1]
AG = MAX_R + NR


def rope_tables():
    theta, factor, hi_ff, lo_ff, orig = 500000.0, 8.0, 4.0, 1.0, 1024
    inv = 1.0 / theta ** (np.arange(0, HD, 2, dtype=np.float64) / HD)
    wavelen = 2.0 * np.pi / inv
    low_wl, high_wl = orig / lo_ff, orig / hi_ff
    smooth = (orig / wavelen - lo_ff) / (hi_ff - lo_ff)
    scaled = np.where(wavelen > low_wl, inv / factor, inv)
    mid = (wavelen <= low_wl) & (wavelen >= high_wl)
    scaled = np.where(mid, (1 - smooth) * inv / factor + smooth * inv, scaled).astype(np.float32)
    freqs = np.arange(T, dtype=np.float32)[:, None] * scaled[None, :]
    emb = np.concatenate([freqs, freqs], axis=-1)
    cos, sin = np.cos(emb).astype(np.float32).T, np.sin(emb).astype(np.float32).T
    sign = np.where(np.arange(HD) < HD // 2, -1.0, 1.0).astype(np.float32)[:, None]
    return np.ascontiguousarray(np.stack([cos, sin * sign], axis=1))


def causal_mask():
    m = np.zeros((P, T), np.float32)
    m[:, T - P:] = np.where(np.arange(P)[None, :] > np.arange(P)[:, None], MASKED, 0.0)
    return m


def fillers(h, place, first):
    wo = lambda *tiles: [] if first else [("wo", t, -1) for t in tiles]
    mod = lambda *which: [("mod", m, 0) for m in which] if first else []
    jobs = {
        (0, 1): [("k", 1, 0)],
        (0, 2): wo(0) + mod(1),
        (0, 3): wo(1),
        (0, 4): wo(2, 3) + [("q", (1, 0), 0)],
        (0, 5): wo(4, 5, 6) + mod(2, 3) + [("q", (1, 1), 0)],
        (1, 1): wo(7),
        (1, 4): [("q", (2, 0), 0)],
        (1, 5): [("q", (2, 1), 0)],
        (2, 4): [("q", (3, 0), 0)],
        (2, 5): [("q", (3, 1), 0)],
        (3, 4): [("q", (0, 0), 1)],
        (3, 5): [("k", 0, 1), ("q", (0, 1), 1), ("v", 0, 1), ("v", 1, 1)],
    }
    return jobs.get((h, place), [])


def parts(i):
    return [range(0, min(i, 3) + 1)] + ([range(4, i + 1)] if i >= 4 else [])


class Numbers:

    def __init__(self):
        self.count = dict.fromkeys("star", 0)
        self.of = {}
        for job in (("mod", 0, 0), ("k", 0, 0), ("q", (0, 0), 0), ("q", (0, 1), 0), ("v", 0, 0), ("v", 1, 0)):
            self.job(job, 0)
        marks = []
        for g in range(GROUPS):
            if g:
                self.back(3, g - 1, first=False)
            for h in range(R):
                self.front(h, g, first=g == 0)
                if h < R - 1:
                    self.back(h, g, first=g == 0)
            marks.append(dict(self.count))
        self.per = {k: marks[2][k] - marks[1][k] for k in "star"}
        assert all(v % 2 == 0 for v in self.per.values())
        self.tail()

    def step(self, kind, name, g):
        self.count[kind] += 1
        self.of[kind, name, g] = self.count[kind]

    def job(self, job, g):
        what, which, ahead = job
        self.step("a", (what, which), g + ahead)
        if what in "qk":
            self.step("r", (what, which), g + ahead)

    def banks(self, h, i, g):
        for part in range(len(parts(i))):
            self.step("t", (h, i, part), g)

    def front(self, h, g, first):
        before = (h - 1, g) if h else (R - 1, g - 1)
        self.step("s", (h, 0), g)
        self.step("s", (h, 1), g)
        for job in fillers(h, 1, first):
            self.job(job, g)
        self.step("s", (h, 2), g)
        if before[1] >= 0:
            self.banks(before[0], 7, before[1])
        self.step("s", (h, 3), g)
        if before[1] >= 0:
            self.job(("pvb", before[0], 0), before[1])
        if h == 0:
            self.step("t", ("v", 0), g)
            self.step("t", ("v", 1), g)

    def back(self, h, g, first, jobs=fillers):
        self.step("s", (h, 4), g)
        for job in jobs(h, 2, first):
            self.job(job, g)
        self.banks(h, 0, g)
        self.banks(h, 1, g)
        self.step("s", (h, 5), g)
        for job in jobs(h, 3, first):
            self.job(job, g)
        self.banks(h, 2, g)
        self.banks(h, 3, g)
        for job in jobs(h, 4, first):
            self.job(job, g)
        self.banks(h, 4, g)
        self.step("s", (h, 6), g)
        self.job(("pva", h, 0), g)
        self.banks(h, 5, g)
        self.step("s", (h, 7), g)
        for job in jobs(h, 5, first):
            self.job(job, g)
        self.banks(h, 6, g)

    def tail(self):
        g = GROUPS - 1
        self.step("s", (3, 4), g)
        for k in (0, 1):
            self.step("t", ("W", k), g)
        self.banks(3, 0, g)
        self.banks(3, 1, g)
        self.step("s", (3, 5), g)
        for k in (2, 3):
            self.step("t", ("W", k), g)
        self.banks(3, 2, g)
        self.banks(3, 3, g)
        self.step("t", ("A", 0), g)
        self.step("t", ("B", 0), g)
        self.banks(3, 4, g)
        self.step("s", (3, 6), g)
        self.job(("pva", 3, 0), g)
        self.banks(3, 5, g)
        self.step("s", (3, 7), g)
        self.job(("wo", 0, 0), g)
        self.job(("wo", 1, 0), g)
        self.banks(3, 6, g)
        self.job(("wo", 2, 0), g)
        self.job(("wo", 3, 0), g)
        self.banks(3, 7, g)
        self.job(("pvb", 3, 0), g)
        for t in range(4, NT):
            self.job(("wo", t, 0), g)

    def value(self, kind, name, at, ahead=0):
        if at.turn is None:
            return self.of.get((kind, name, at.g + ahead))
        base = self.of[kind, name, at.g + ahead]
        for turn in range(GROUPS - 1):
            assert self.of[kind, name, at.g + ahead + turn] == base + self.per[kind] * turn
        return base + at.turn * self.per[kind]

    def slot(self, kind, name, at, ahead=0):
        return (self.of[kind, name, at.g + ahead] - 1) % 2


    def last(self, kind, at, *steps):
        def base(step):
            return self.of.get((kind, step[0], at.g + step[1]), -9) - step[2]
        name, ahead, less = max(steps, key=base)
        return back_of(self.value(kind, name, at, ahead), less)


class Group:

    def __init__(self, g, turn=None):
        self.g, self.turn = g, turn

    @property
    def index(self):
        return self.g if self.turn is None else self.g + self.turn

    @property
    def first(self):
        return self.g == 0


def back_of(n, k):
    if n is None or k == 0:
        return n
    if isinstance(n, int):
        return n - k if n > k else None
    return n - k


def need(engine, semaphore, value):
    if value is not None:
        engine.wait_ge(semaphore, value)


def need_apart(engine, passed, *waits):
    for semaphore, n in waits:
        need(engine, semaphore, n)
    engine.sem_inc(passed, 1)


def adaln_block(nc, x, wq, wk, wv, wo, ffn_w, ffn_b, ffn_a, ffn_bb, gate_w, gate_b, c, wmod, out):
    N = Numbers()
    trig_c = nc.inline_tensor(rope_tables(), name="rope_tables").ap()
    mask_c = nc.inline_tensor(causal_mask(), name="causal_mask").ap()
    ident_c = nc.inline_tensor(np.eye(P, dtype=np.float32), name="identity").ap()

    with ExitStack() as ctx:
        sb = lambda name, shape, dt=F32: ctx.enter_context(nc.sbuf_tensor(name, shape, dt))
        sem = lambda name: ctx.enter_context(nc.semaphore(name))

        h_hi, h_lo = sb("h_hi", [P, KC, T], F32R), sb("h_lo", [P, KC, T], F32R)
        k_hi, k_lo = sb("k_hi", [P, T], F32R), sb("k_lo", [P, T], F32R)
        q_hi, q_lo = sb("q_hi", [P, T], F32R), sb("q_lo", [P, T], F32R)
        v_hi, v_lo = sb("v_hi", [P, NT, HD], F32R), sb("v_lo", [P, NT, HD], F32R)
        pa_hi, pa_lo = sb("pa_hi", [P, 13, P], F32R), sb("pa_lo", [P, 13, P], F32R)
        pb_hi, pb_lo = sb("pb_hi", [P, 29, P], F32R), sb("pb_lo", [P, 29, P], F32R)
        o_hi, o_lo = sb("o_hi", [P, R, T], F32R), sb("o_lo", [P, R, T], F32R)
        wq_hi, wq_lo = sb("wq_hi", [P, KC, HD], F32R), sb("wq_lo", [P, KC, HD], F32R)
        wk_hi, wk_lo = sb("wk_hi", [P, KC, HD], F32R), sb("wk_lo", [P, KC, HD], F32R)
        wv_hi, wv_lo = sb("wv_hi", [P, KC, HD], F32R), sb("wv_lo", [P, KC, HD], F32R)
        wo_hi, wo_lo = sb("wo_hi", [P, R, D], F32R), sb("wo_lo", [P, R, D], F32R)
        y = sb("y", [P, NT, D])
        trig = sb("trig", [P, 2, T])
        mask = sb("mask", [P, T])
        ident = sb("ident", [P, P])
        stage = sb("stage", [P, 2, D])
        qc = sb("qc", [P, 2, HALF])
        qr = sb("qr", [P, 2, HALF])
        vt = sb("vt", [P, T])
        p_small = sb("p_small", [P, 1280])
        p_large = sb("p_large", [P, 2, T])
        ga_b, gb_b = sb("ga_b", [P, D]), sb("gb_b", [P, D])
        silu = sb("silu", [P, 4, KC])
        modc = sb("modc", [P, 4, KC])
        negmax, rowsum, rowinv = sb("negmax", [P, NT]), sb("rowsum", [P, NT]), sb("rowinv", [P, NT])
        stats, mv, rstd = sb("stats", [P, NT, 6]), sb("mv", [P, NT, 2]), sb("rstd", [P, NT])
        gate_bb = sb("gate_bb", [P, NR])
        gs = sb("gs", [P, 2, 10, NR])

        S = ctx.enter_context(nc.psum_tensor("scores", [P, 4, HALF], F32))
        TB = ctx.enter_context(nc.psum_tensor("transposed", [P, 2, HALF], F32))
        ACC = ctx.enter_context(nc.psum_tensor("accumulators", [P, 2, HALF], F32))
        S_flat = S[:].rearrange("p b n -> p (b n)")

        c_in, ident_in, tab_in = sem("c_in"), sem("ident_in"), sem("tab_in")
        x_in = [sem(f"x_in{t}") for t in range(NT)]
        mod_in = sem("mod_in")
        stage_in = [sem("stage_in0"), sem("stage_in1")]
        silu_done_exp, silu_done, y_zero = sem("silu_done_exp"), sem("silu_done"), sem("y_zero")
        ln_stat, ln_std, ln_inv, xn_done = sem("ln_stat"), sem("ln_std"), sem("ln_inv"), sem("xn_done")
        xt_full, h_f32, h_hi_done, h_done = sem("xt_full"), sem("h_f32"), sem("h_hi_done"), sem("h_done")
        zeroed = sem("zeroed")
        s_full, s_masked, s_exp, s_inv, s_norm = (sem(n) for n in ("s_full", "s_masked", "s_exp", "s_inv", "s_norm"))
        t_full, t_hi, t_lo = sem("t_full"), sem("t_hi"), sem("t_lo")
        a_full, a_hi, a_swapped, a_taken = sem("a_full"), sem("a_hi"), sem("a_swapped"), sem("a_taken")
        r_sin, r_sum, r_hi, r_lo = sem("r_sin"), sem("r_sum"), sem("r_hi"), sem("r_lo")
        w_hi, w_lo = sem("w_hi"), sem("w_lo")
        vec = sem("vec")
        dve_passed, pool_passed = sem("dve_passed"), sem("pool_passed")
        f_in, f_low_in, f_x = sem("f_in"), sem("f_low_in"), [sem(f"x_back{s}") for s in range(4)]
        f_ga, f_x2, f_stat, f_std, f_xn = (sem(n) for n in ("f_ga", "f_x2", "f_stat", "f_std", "f_xn"))
        f_tr, f_aff, f_affv, f_hi, f_lo = (sem(n) for n in ("f_tr", "f_aff", "f_affv", "f_hi", "f_lo"))
        f_gate, f_ffn, f_smax, f_exp, f_tm = (sem(n) for n in ("f_gate", "f_ffn", "f_smax", "f_exp", "f_tm"))
        f_tmt, f_tmhi, f_tmlo, f_full = (sem(n) for n in ("f_tmt", "f_tmhi", "f_tmlo", "f_full"))
        f_sum, f_gb, f_out, stored = (sem(n) for n in ("f_sum", "f_gb", "f_out", "stored"))
        b_in = sem("b_in")

        def row(i, n=None):
            n = n or P * (i + 1)
            if i < 4:
                at = (0, 128, 384, 768)[i]
                return p_small[:, at:at + n]
            return p_large[:, i % 2, 0:n]

        def score_at(i):
            if i < 4:
                return HALF * i
            return (0, 2 * HALF)[i % 2] + (P if i == 4 else 0)

        PIECES = {0: [256], 1: [256], 2: [384], 3: [512], 4: [384, 256], 5: [512, 256], 6: [512, 384], 7: [512, 512]}
        SCORES_BEFORE = {0: (1, 6), 1: (1, 6), 2: (1, 7), 3: (1, 7), 4: (0, 1), 5: (0, 3), 6: (0, 4), 7: (0, 5)}

        def pt_of(i, part, hi):
            js = parts(i)[part]
            n = len(js)
            if i < 4:
                buf = pa_hi if hi else pa_lo
                return buf[:, i:i + 3 * (n - 1) + 1:3, :]
            buf = pb_hi if hi else pb_lo
            if part == 0:
                return buf[:, i - 4:i - 4 + 4 * (n - 1) + 1:4, :]
            at = 16 + i - 4
            return buf[:, at:at + 3 * (n - 1) + 1:3, :]

        def pt_row(j, half, hi):
            if half == 0:
                i0 = min(j, 2)
                buf, at = (pa_hi if hi else pa_lo), 3 * j + i0
                return i0 * P, buf[:, at:at + 4 - i0, :].rearrange("p a b -> p (a b)")
            buf = pb_hi if hi else pb_lo
            if j < 4:
                return 0, buf[:, 4 * j:4 * j + 4, :].rearrange("p a b -> p (a b)")
            i0 = min(j - 4, 2)
            at = 16 + 3 * (j - 4) + i0
            return i0 * P, buf[:, at:at + 4 - i0, :].rearrange("p a b -> p (a b)")

        def x_tile(t):
            return (qc, qr)[t // 2][:, t % 2, :] if t < 4 else p_large[:, (t - 4) // 2, (t % 2) * D:(t % 2 + 1) * D]

        def f32(ap):
            return ap.bitcast(F32)

        def before(h, at):
            return (h - 1, 0) if h else (R - 1, -1)

        W_FIRST = [("k", 0), ("q", 0), ("v", 0)]
        W_GROUP = [("q", 1), ("q", 2), ("wo", 0), ("q", 3), ("wo", 1), ("wo", 2), ("wo", 3)]
        W_NEXT = [("q", 0), ("k", 0), ("v", 0)]
        W_PER = len(W_GROUP) + len(W_NEXT)

        def w_number(what, at, ahead=0):
            if what in W_GROUP:
                base = len(W_FIRST) + W_GROUP.index(what) + 1 + W_PER * (at.g + ahead)
            elif at.g + ahead == 0:
                base = W_FIRST.index(what) + 1
            else:
                base = len(W_FIRST) + len(W_GROUP) + W_NEXT.index(what) + 1 + W_PER * (at.g + ahead - 1)
            return base if at.turn is None else base + at.turn * W_PER

        def w_slot(what, at, ahead=0):
            return (w_number(what, Group(at.g), ahead) - 1) % 2

        def stage_count(what, at, ahead=0):
            n = w_number(what, Group(at.g), ahead)
            value = 16 * ((n + 1) // 2)
            return value if at.turn is None else value + at.turn * (16 * W_PER // 2)

        y_flat = y[:].rearrange("p t n -> p (t n)")
        mod_w = y_flat.rearrange("p (k n) -> p k n", k=KC)

        fw_hi, fw_lo = h_hi[:, :, 0:D], h_lo[:, :, 0:D]
        h2_hi = lambda s: h_hi[:, s, D:T].rearrange("p (k n) -> p k n", k=KC)
        h2_lo = lambda s: h_lo[:, s, D:T].rearrange("p (k n) -> p k n", k=KC)
        fb_hi, fb_lo = h_hi[0:MAX_R, 2, D:T], h_lo[0:MAX_R, 2, D:T]
        tm_hi = lambda s: h_hi[0:MAX_R, 3, D + P * s:D + P * (s + 1)]
        tm_lo = lambda s: h_lo[0:MAX_R, 3, D + P * s:D + P * (s + 1)]
        fw_in = trig[:].rearrange("p a (b n) -> p (a b) n", b=2)
        ag_in = stage[0:AG, 0, :]
        fb_in = stage[:, 1, 0:KC * MAX_R].rearrange("p (k n) -> p k n", k=KC)
        ag_t = vt[:, 0:KC * AG].rearrange("p (k n) -> p k n", k=KC)
        tm = lambda s: vt[:, 512 + MAX_R * s:512 + MAX_R * (s + 1)]
        x_again = lambda t: (qc, qr)[(t % 4) // 2][:, t % 2, :]
        xn2 = lambda s: p_small[:, D * s:D * (s + 1)]
        h2_f = lambda s: trig[:, s, 0:D]
        f_tmp = lambda s: trig[:, s, D:T]
        ffn_bias = mask[:, 0:D]

        G7 = Group(GROUPS - 1)
        block = ctx.enter_context(nc.Block())

        @block.sync
        def _(sp):
            x_v = x[0].rearrange("(t p) d -> t p d", p=P)
            wmod_v = wmod.rearrange("(k p) n -> p k n", p=P)
            sp.dma_start(silu[:, 0, :], c.rearrange("o (k p) -> p (o k)", p=P), allow_slow_non_contiguous=True).then_inc(c_in, 16)
            for t in range(NT // 2):
                sp.dma_start(x_tile(t), x_v[t]).then_inc(x_in[t], 16)
            sp.dma_start(ident[:], ident_c).then_inc(ident_in, 16)
            sp.dma_start(mod_w, wmod_v[:, :, 0:2 * D]).then_inc(mod_in, 16)
            for t in range(NT // 2, NT):
                sp.dma_start(x_tile(t), x_v[t]).then_inc(x_in[t], 16)

            weights = {"q": (wq, R), "k": (wk, 1), "v": (wv, 1)}

            def load(what, at, ahead=0):
                kind, r = what
                s = w_slot(what, at, ahead)
                need(sp, w_lo, back_of(w_number(what, at, ahead), 2))
                if kind == "wo":
                    src = wo[bass.ds(((at.index + ahead) * R + r) * HD, HD), :]
                    dst = stage[:, s, :]
                else:
                    w, per = weights[kind]
                    src = w.rearrange("(k p) n -> p k n", p=P)[:, :, bass.ds(((at.index + ahead) * per + r) * HD, HD)]
                    dst = stage[:, s, :].rearrange("p (k n) -> p k n", k=KC)
                sp.dma_start(dst, src).then_inc(stage_in[s], 16)

            g0 = Group(0)
            load(("k", 0), g0)
            load(("q", 0), g0)
            sp.dma_start(trig[:], trig_c).then_inc(tab_in, 16)
            load(("v", 0), g0)
            sp.dma_start(mask[:], mask_c).then_inc(tab_in, 16)
            sp.wait_ge(a_full, N.value("a", ("mod", 0), g0))
            sp.dma_start(mod_w, wmod_v[:, :, 3 * D:5 * D]).then_inc(mod_in, 16)
            load(("q", 1), g0)
            sp.wait_ge(a_full, N.value("a", ("mod", 1), g0))
            sp.dma_start(mod_w[:, :, 0:D], wmod_v[:, :, 2 * D:3 * D]).then_inc(mod_in, 16)
            sp.dma_start(mod_w[:, :, D:2 * D], wmod_v[:, :, 5 * D:6 * D]).then_inc(mod_in, 16)
            for what in W_GROUP[1:]:
                load(what, g0)
            with sp.Fori(0, GROUPS - 1) as turn:
                at = Group(1, turn)
                for what in W_NEXT:
                    load(what, at)
                for what in W_GROUP:
                    load(what, at)

            sp.wait_ge(r_sum, N.value("r", ("q", (3, 1)), G7))
            sp.wait_ge(a_taken, N.value("a", ("q", (3, 1)), G7))
            sp.dma_start(fw_in, ffn_w.rearrange("(o p) i -> p o i", p=P)).then_inc(f_in, 16)
            sp.wait_ge(w_lo, w_number(("wo", 3), G7))
            sp.dma_start(stage[0:MAX_R, 0, :], ffn_a).then_inc(f_low_in, 16)
            sp.dma_start(stage[MAX_R:AG, 0, :], gate_w).then_inc(f_low_in, 16)
            sp.dma_start(fb_in, ffn_bb.rearrange("(k p) r -> p k r", p=P)).then_inc(f_low_in, 16)
            sp.dma_start(gate_bb[:], gate_b.rearrange("(o r) -> o r", o=1).to_broadcast([P, NR])).then_inc(b_in, 16)
            sp.wait_ge(r_lo, N.value("r", ("q", (3, 1)), G7))
            for t in range(NT):
                if t >= 4:
                    sp.wait_ge(f_x2, t - 3)
                sp.dma_start(x_again(t), x_v[t]).then_inc(f_x[t % 4], 16)
                if t == 3:
                    sp.wait_ge(s_masked, N.value("s", (3, 7), G7))
                    sp.dma_start(ffn_bias, ffn_b.rearrange("(o n) -> o n", o=1).to_broadcast([P, D])).then_inc(b_in, 16)
            for t in range(NT):
                sp.wait_ge(f_out, t + 1)
                sp.dma_start(out[0].rearrange("(t p) d -> t p d", p=P)[t], y[:, t, :]).then_inc(stored, 16)
            sp.wait_ge(stored, 16 * NT)

        @block.tensor
        def _(pe):
            def scores(h, i, at):
                back, tile = SCORES_BEFORE[i]
                hb, ahead = (h, 0) if not back else before(h, at)
                need(pe, s_masked, N.value("s", (hb, tile), at, ahead))
                half = i // 4
                need(pe, r_lo, N.last("r", at, (("q", (h, half)), 0, 0), (("k", half), 0, 0)))
                c0 = score_at(i)
                key = 0
                for n in PIECES[i]:
                    for k, (a, b) in enumerate(((q_hi, k_hi), (q_hi, k_lo), (q_lo, k_hi))):
                        mm = nc.tensor.matmul(S_flat[:, c0 + key:c0 + key + n], a[:, i * P:(i + 1) * P],
                                              b[:, key:key + n], start=(k == 0), stop=(k == 2))
                    key += n
                mm.then_inc(s_full, 1)

            def transposes(h, i, at, ahead=0):
                need(pe, s_norm, N.value("s", (h, i), at, ahead))
                for part, js in enumerate(parts(i)):
                    name = (h, i, part)
                    b = N.slot("t", name, at, ahead)
                    need(pe, t_lo, back_of(N.value("t", name, at, ahead), 2))
                    for j in js:
                        mm = nc.tensor.transpose(TB[:, b, (j % 4) * P:(j % 4 + 1) * P], row(i)[:, j * P:(j + 1) * P], ident[:])
                    mm.then_inc(t_full, 1)

            def bank_free(name, at, ahead):
                need(pe, a_taken, back_of(N.value("a", name, at, ahead), 2))

            def weighted(h, half, at, ahead=0):
                name = (("pva", "pvb")[half], h)
                bank_free(name, at, ahead)
                acc = ACC[:, N.slot("a", name, at, ahead), :]
                hi_lo = [(v_hi, True), (v_lo, True), (v_hi, False)]
                if half == 0:
                    steps = [(t_lo, (h, 3, 0), hi_lo, range(4))]
                else:
                    steps = [(t_hi, (h, 7, 0), hi_lo[:2], range(4)), (t_lo, (h, 7, 0), hi_lo[2:], range(4)),
                             (t_lo, (h, 7, 1), hi_lo, range(4, 8))]
                for done, tiles, products, keys in steps:
                    need(pe, done, N.value("t", tiles, at, ahead))
                    for v, hi in products:
                        for j in keys:
                            c0, pt = pt_row(j, half, hi)
                            mm = nc.tensor.matmul(acc[:, c0:HALF], v[:, j, :], pt, start=(hi and v is v_hi and j == 0),
                                                  stop=(not hi and j == 4 * half + 3))
                mm.then_inc(a_full, 1)

            def project(name, at, ahead=0):
                kind, which = name
                head, half = which if kind == "q" else (0, which)
                bank_free(name, at, ahead)
                pe.wait_ge(w_lo, w_number((kind, head), at, ahead))
                w, w_rest = {"q": (wq_hi, wq_lo), "k": (wk_hi, wk_lo), "v": (wv_hi, wv_lo)}[kind]
                acc = ACC[:, N.slot("a", name, at, ahead), :]
                n = 0
                for a, b in ((w, h_hi), (w, h_lo), (w_rest, h_hi)):
                    for k in range(KC):
                        mm = nc.tensor.matmul(acc, a[:, k, :], b[:, k, half * HALF:(half + 1) * HALF],
                                              start=(n == 0), stop=(n == 3 * KC - 1))
                        n += 1
                mm.then_inc(a_full, 1)

            def project_out(t, at, ahead):
                name = ("wo", t)
                need(pe, a_taken, N.last("a", at, (name, ahead, 2), ((("pva", "pvb")[t // 4], R - 1), ahead, 0)))
                pe.wait_ge(w_lo, w_number(("wo", R - 1), at, ahead))
                acc = ACC[:, N.slot("a", name, at, ahead), :]
                n = 0
                for a, b in ((o_hi, wo_hi), (o_hi, wo_lo), (o_lo, wo_hi)):
                    for r in range(R):
                        mm = nc.tensor.matmul(acc, a[:, r, t * P:(t + 1) * P], b[:, r, :],
                                              start=(n == 0), stop=(n == 3 * R - 1))
                        n += 1
                mm.then_inc(a_full, 1)

            def modulation(m, at):
                name = ("mod", m)
                bank_free(name, at, 0)
                pe.wait_ge(mod_in, 16 * (m + 1) if m < 2 else 64)
                acc = ACC[:, N.slot("a", name, at), :]
                if m < 2:
                    if m == 0:
                        pe.wait_ge(silu_done, 1)
                    for n in range(2 * KC):
                        for k in range(KC):
                            mm = nc.tensor.matmul(acc[:, n:n + 1], mod_w[:, k, n * P:(n + 1) * P],
                                                  silu[:, 3, k:k + 1], start=(k == 0), stop=(k == KC - 1))
                else:
                    pe.wait_ge(silu_done, 2)
                    for k in range(KC):
                        mm = nc.tensor.matmul(acc, vt[:, k * P:(k + 1) * P], mod_w[:, k, (m - 2) * D:(m - 1) * D],
                                              start=(k == 0), stop=(k == KC - 1))
                mm.then_inc(a_full, 1)

            def value_transposes(half, at):
                name = ("v", half)
                b = N.slot("t", name, at)
                need(pe, t_lo, back_of(N.value("t", name, at), 2))
                need(pe, a_taken, N.value("a", ("v", half), at))
                for j in range(4):
                    c0 = half * HALF + j * P
                    mm = nc.tensor.transpose(TB[:, b, j * P:(j + 1) * P], vt[:, c0:c0 + P], ident[:])
                mm.then_inc(t_full, 1)

            def fill(h, place, at):
                for what, which, ahead in fillers(h, place, at.first):
                    if what == "wo":
                        project_out(which, at, ahead)
                    elif what == "mod":
                        modulation(which, at)
                    else:
                        project((what, which), at, ahead)

            def front(h, at):
                hb, ahead = before(h, at)
                scores(h, 0, at)
                scores(h, 1, at)
                fill(h, 1, at)
                scores(h, 2, at)
                if h or not at.first:
                    transposes(hb, 7, at, ahead)
                scores(h, 3, at)
                if h or not at.first:
                    weighted(hb, 1, at, ahead)
                if h == 0:
                    value_transposes(0, at)
                    value_transposes(1, at)

            def back(h, at):
                scores(h, 4, at)
                fill(h, 2, at)
                transposes(h, 0, at)
                transposes(h, 1, at)
                scores(h, 5, at)
                fill(h, 3, at)
                transposes(h, 2, at)
                transposes(h, 3, at)
                fill(h, 4, at)
                transposes(h, 4, at)
                scores(h, 6, at)
                weighted(h, 0, at)
                transposes(h, 5, at)
                scores(h, 7, at)
                fill(h, 5, at)
                transposes(h, 6, at)

            g0 = Group(0)
            pe.wait_ge(ident_in, 16)
            for half in range(2):
                for k in range(KC):
                    if k == 0:
                        pe.wait_ge(xn_done, 4 * (half + 1))
                    if half:
                        pe.wait_ge(h_f32, k + 1)
                    for t in range(4):
                        mm = nc.tensor.transpose(S[:, k, t * P:(t + 1) * P],
                                                 x_tile(4 * half + t)[:, k * P:(k + 1) * P], ident[:])
                    mm.then_inc(xt_full, 1)
                if half == 0:
                    modulation(0, g0)
            pe.wait_ge(h_done, KC)
            project(("k", 0), g0)
            project(("q", (0, 0)), g0)
            pe.wait_ge(h_done, 2 * KC)
            project(("q", (0, 1)), g0)
            project(("v", 0), g0)
            project(("v", 1), g0)

            for h in range(R - 1):
                front(h, g0)
                back(h, g0)
            front(R - 1, g0)
            with pe.Fori(0, GROUPS - 1) as turn:
                at = Group(1, turn)
                back(R - 1, Group(0, turn))
                for h in range(R - 1):
                    front(h, at)
                    back(h, at)
                front(R - 1, at)

            def tail_bank(name):
                b = N.slot("t", name, G7)
                pe.wait_ge(t_lo, N.value("t", name, G7) - 2)
                return TB[:, b, :]

            def weight_transposes(k):
                bank = tail_bank(("W", k))
                for o in range(KC):
                    mm = nc.tensor.transpose(bank[:, o * P:(o + 1) * P], fw_in[:, o, k * P:(k + 1) * P], ident[:])
                mm.then_inc(t_full, 1)

            scores(3, 4, G7)
            pe.wait_ge(f_in, 16)
            weight_transposes(0)
            weight_transposes(1)
            transposes(3, 0, G7)
            transposes(3, 1, G7)
            scores(3, 5, G7)
            weight_transposes(2)
            weight_transposes(3)
            transposes(3, 2, G7)
            transposes(3, 3, G7)
            pe.wait_ge(f_low_in, 16 * 3)
            bank = tail_bank(("A", 0))
            for k in range(KC):
                mm = nc.tensor.transpose(bank[:, k * AG:(k + 1) * AG], ag_in[:, k * P:(k + 1) * P], ident[0:AG, 0:AG])
            mm.then_inc(t_full, 1)
            bank = tail_bank(("B", 0))
            for o in range(KC):
                mm = nc.tensor.transpose(bank[0:MAX_R, o * P:(o + 1) * P], fb_in[:, o, :], ident[:])
            mm.then_inc(t_full, 1)
            transposes(3, 4, G7)
            scores(3, 6, G7)
            weighted(3, 0, G7)
            transposes(3, 5, G7)
            scores(3, 7, G7)
            project_out(0, G7, 0)
            project_out(1, G7, 0)
            transposes(3, 6, G7)
            project_out(2, G7, 0)
            project_out(3, G7, 0)
            transposes(3, 7, G7)
            weighted(3, 1, G7)
            for t in range(NT // 2, NT):
                project_out(t, G7, 0)

            def spread(t):
                s = t % 2
                pe.wait_ge(f_xn, t + 1)
                if t == 0:
                    pe.wait_ge(s_masked, N.value("s", (3, 7), G7))
                if t >= 2:
                    pe.wait_ge(f_aff, 2 * (t - 1))
                    pe.wait_ge(f_affv, t - 1)
                for k in range(KC):
                    mm = nc.tensor.transpose(S[:, 2 + s, k * P:(k + 1) * P], xn2(s)[:, k * P:(k + 1) * P], ident[:])
                mm.then_inc(f_tr, 1)

            def feed(t):
                s = t % 2
                pe.wait_ge(f_aff, 2 * (t + 1))
                pe.wait_ge(f_affv, t + 1)
                if t == 0:
                    pe.wait_ge(t_lo, N.count["t"])
                if t >= 2:
                    pe.wait_ge(f_tmlo, t - 1)
                for k in range(KC):
                    mm = nc.tensor.matmul(TB[:, s, 0:AG], h2_f(s)[:, k * P:(k + 1) * P], ag_t[:, k, :],
                                          start=(k == 0), stop=(k == KC - 1))
                mm.then_inc(f_gate, 1)
                pe.wait_ge(f_lo, t + 1)
                if t >= 2:
                    pe.wait_ge(f_sum, t - 1)
                n = 0
                for a, b in ((h2_hi(s), fw_hi), (h2_hi(s), fw_lo), (h2_lo(s), fw_hi)):
                    for k in range(KC):
                        mm = nc.tensor.matmul(S[:, s, :], a[:, k, :], b[:, k, :], start=(n == 0), stop=False)
                        n += 1
                mm.then_inc(f_ffn, 1)

            def low_rank(t):
                s = t % 2
                pe.wait_ge(f_tm, t + 1)
                nc.tensor.transpose(TB[0:MAX_R, s, 2 * P:3 * P], tm(s), ident[:]).then_inc(f_tmt, 1)
                pe.wait_ge(f_tmlo, t + 1)
                for n, (a, b) in enumerate(((tm_hi(s), fb_hi), (tm_hi(s), fb_lo), (tm_lo(s), fb_hi))):
                    mm = nc.tensor.matmul(S[:, s, :], a, b, start=False, stop=(n == 2))
                mm.then_inc(f_full, 1)

            for t in range(NT + 1):
                if t < NT:
                    spread(t)
                if t >= 1:
                    low_rank(t - 1)
                if t < NT:
                    feed(t)

        @block.scalar
        def _(act):
            def exp(h, i, at):
                need(act, s_masked, N.value("s", (h, i), at))
                nc.scalar.activation(row(i), row(i), ACT.Exp, bias=negmax[:, i:i + 1], scale=-1.0,
                                     accum_out=rowsum[:, i:i + 1]).then_inc(s_exp, 1)

            def transposed_hi(h, i, at, ahead=0):
                for part, js in enumerate(parts(i)):
                    name = (h, i, part)
                    need(act, t_full, N.value("t", name, at, ahead))
                    src = TB[:, N.slot("t", name, at, ahead), 0:len(js) * P].rearrange("p (a b) -> p a b", b=P)
                    nc.scalar.activation(pt_of(i, part, True), src, ACT.Copy).then_inc(t_hi, 1)

            def value_hi(half, at):
                name = ("v", half)
                need(act, t_full, N.value("t", name, at))
                src = TB[:, N.slot("t", name, at), :].rearrange("p (a b) -> p a b", b=P)
                nc.scalar.activation(v_hi[:, 4 * half:4 * half + 4, :], src, ACT.Copy).then_inc(t_hi, 1)

            def output_hi(h, half, at, ahead=0):
                name = (("pva", "pvb")[half], h)
                need(act, a_full, N.value("a", name, at, ahead))
                nc.scalar.activation(o_hi[:, h, half * HALF:(half + 1) * HALF],
                                     ACC[:, N.slot("a", name, at, ahead), :], ACT.Copy).then_inc(a_hi, 1)

            def swap_halves(name, at, ahead=0):
                need(act, a_full, N.value("a", name, at, ahead))
                need(act, r_sum, back_of(N.value("r", name, at, ahead), 2))
                acc = ACC[:, N.slot("a", name, at, ahead), :]
                dst = qr[:, N.slot("r", name, at, ahead), :]
                nc.scalar.activation(dst[0:HD // 2, :], acc[HD // 2:HD, :], ACT.Copy)
                nc.scalar.activation(dst[HD // 2:HD, :], acc[0:HD // 2, :], ACT.Copy).then_inc(a_swapped, 1)

            def rotated_hi(name, at, ahead=0):
                kind, which = name
                need(act, r_sum, N.value("r", name, at, ahead))
                if kind == "k" and which == 0:
                    need(act, s_full, N.value("s", (R - 1, 7), at, ahead - 1))
                dst, half = (q_hi, which[1]) if kind == "q" else (k_hi, which)
                nc.scalar.activation(dst[:, half * HALF:(half + 1) * HALF], qc[:, N.slot("r", name, at, ahead), :],
                                     ACT.Copy).then_inc(r_hi, 1)

            def split_hi(what, at, ahead=0):
                kind, r = what
                s = w_slot(what, at, ahead)
                act.wait_ge(stage_in[s], stage_count(what, at, ahead))
                if kind == "wo":
                    last_use = (("wo", NT - 1), ahead - 1)
                else:
                    last_use = (("q", (r - 1 if r else R - 1, 1)), ahead if r else ahead - 1)
                need(act, a_full, N.value("a", last_use[0], at, last_use[1]))
                dst = {"q": wq_hi, "k": wk_hi, "v": wv_hi}.get(kind)
                dst = wo_hi[:, r, :] if kind == "wo" else dst[:].rearrange("p k n -> p (k n)")
                nc.scalar.activation(dst, stage[:, s, :], ACT.Copy).then_inc(w_hi, 1)

            def fill(h, place, at, jobs=slice(None)):
                for what, which, ahead in fillers(h, place, at.first)[jobs]:
                    if what in "qk":
                        swap_halves((what, which), at, ahead)

            def front(h, at):
                hb, ahead = before(h, at)
                exp(h, 0, at)
                exp(h, 1, at)
                fill(h, 1, at)
                if h or not at.first:
                    transposed_hi(hb, 7, at, ahead)
                exp(h, 2, at)
                exp(h, 3, at)
                if h or not at.first:
                    rotated_hi(("q", (h, 1)), at)
                if h == 0:
                    rotated_hi(("k", 1), at)
                if h < R - 1:
                    split_hi(("q", h + 1), at)
                else:
                    split_hi(("wo", 3), at)
                if h or not at.first:
                    output_hi(hb, 1, at, ahead)
                if h == 0:
                    value_hi(0, at)
                    value_hi(1, at)

            def back(h, at):
                last = h == R - 1
                transposed_hi(h, 0, at)
                transposed_hi(h, 1, at)
                if last:
                    split_hi(("q", 0), at, 1)
                exp(h, 4, at)
                transposed_hi(h, 2, at)
                transposed_hi(h, 3, at)
                exp(h, 5, at)
                if h == 1:
                    split_hi(("wo", 0), at)
                if h == 2:
                    split_hi(("wo", 1), at)
                fill(h, 4, at)
                transposed_hi(h, 4, at)
                if last:
                    split_hi(("k", 0), at, 1)
                exp(h, 6, at)
                output_hi(h, 0, at)
                transposed_hi(h, 5, at)
                rotated_hi(("q", ((h + 1) % R, 0)), at, int(last))
                exp(h, 7, at)
                if h == 2:
                    split_hi(("wo", 2), at)
                if last:
                    split_hi(("v", 0), at, 1)
                fill(h, 5, at, slice(0, -1))
                if last:
                    rotated_hi(("k", 0), at, 1)
                transposed_hi(h, 6, at)
                fill(h, 5, at, slice(-1, None))

            g0 = Group(0)
            for half in range(2):
                act.wait_ge(ln_stat, half + 1)
                nc.scalar.activation(rstd[:, 4 * half:4 * half + 4], rstd[:, 4 * half:4 * half + 4],
                                     ACT.Sqrt).then_inc(ln_std, 1)
            act.wait_ge(c_in, 16)
            nc.scalar.activation(silu[:, 1, :], silu[:, 0, :], ACT.Exp, scale=-1.0).then_inc(silu_done_exp, 1)
            for what in W_FIRST[:2]:
                split_hi(what, g0)
            for n in range(2 * KC):
                act.wait_ge(h_f32, n + 1)
                half, k = divmod(n, KC)
                nc.scalar.activation(h_hi[:, k, half * HALF:(half + 1) * HALF], vt[:, (n % 2) * HALF:(n % 2 + 1) * HALF],
                                     ACT.Copy).then_inc(h_hi_done, 1)
            swap_halves(("k", 0), g0)
            swap_halves(("q", (0, 0)), g0)
            rotated_hi(("k", 0), g0)
            split_hi(W_FIRST[2], g0)
            rotated_hi(("q", (0, 0)), g0)
            swap_halves(("q", (0, 1)), g0)
            rotated_hi(("q", (0, 1)), g0)
            for h in range(R - 1):
                front(h, g0)
                back(h, g0)
            front(R - 1, g0)
            with act.Fori(0, GROUPS - 1) as turn:
                at = Group(1, turn)
                back(R - 1, Group(0, turn))
                for h in range(R - 1):
                    front(h, at)
                    back(h, at)
                front(R - 1, at)

            def weight_hi(name, dst, rows=P):
                act.wait_ge(t_full, N.value("t", name, G7))
                nc.scalar.activation(dst, TB[0:rows, N.slot("t", name, G7), :], ACT.Copy).then_inc(t_hi, 1)

            weight_hi(("W", 0), fw_hi[:, 0, :])
            weight_hi(("W", 1), fw_hi[:, 1, :])
            transposed_hi(3, 0, G7)
            transposed_hi(3, 1, G7)
            exp(3, 4, G7)
            weight_hi(("W", 2), fw_hi[:, 2, :])
            weight_hi(("W", 3), fw_hi[:, 3, :])
            transposed_hi(3, 2, G7)
            transposed_hi(3, 3, G7)
            exp(3, 5, G7)
            act.wait_ge(t_full, N.value("t", ("A", 0), G7))
            nc.scalar.activation(vt[:, 0:KC * AG], TB[:, N.slot("t", ("A", 0), G7), 0:KC * AG], ACT.Copy).then_inc(t_hi, 1)
            weight_hi(("B", 0), fb_hi, MAX_R)
            transposed_hi(3, 4, G7)
            exp(3, 6, G7)
            output_hi(3, 0, G7)
            transposed_hi(3, 5, G7)
            exp(3, 7, G7)
            transposed_hi(3, 6, G7)
            transposed_hi(3, 7, G7)
            output_hi(3, 1, G7)

            def router_exp(t):
                s = t % 2
                act.wait_ge(f_smax, t + 1)
                nc.scalar.activation(gs[:, s, 2, :], gs[:, s, 0, :], ACT.Exp, bias=gs[:, s, 1, 1:2],
                                     accum_out=gs[:, s, 1, 2:3]).then_inc(f_exp, 1)

            for t in range(NT + 1):
                if t < NT:
                    s = t % 2
                    act.wait_ge(f_stat, t + 1)
                    nc.scalar.activation(rstd[:, t:t + 1], rstd[:, t:t + 1], ACT.Sqrt).then_inc(f_std, 1)
                    act.wait_ge(f_tr, t + 1)
                    if t >= 2:
                        act.wait_ge(f_ffn, t - 1)
                    for k in range(KC // 2):
                        nc.scalar.activation(h2_f(s)[:, k * P:(k + 1) * P], S[:, 2 + s, k * P:(k + 1) * P], ACT.Identity,
                                             bias=modc[:, 2, k:k + 1], scale=modc[:, 3, k:k + 1]).then_inc(f_aff, 1)
                    act.wait_ge(f_aff, 2 * (t + 1))
                    act.wait_ge(f_affv, t + 1)
                    nc.scalar.activation(h2_hi(s).rearrange("p k n -> p (k n)"), h2_f(s), ACT.Copy).then_inc(f_hi, 1)
                if t >= 1:
                    s = (t - 1) % 2
                    act.wait_ge(f_tmt, t)
                    nc.scalar.activation(tm_hi(s), TB[0:MAX_R, s, 2 * P:3 * P], ACT.Copy).then_inc(f_tmhi, 1)
                if t < NT:
                    router_exp(t)

        @block.vector
        def _(dve):
            linked = [0]

            def link(ins):
                linked[0] += 1
                ins.then_inc(vec, 1)
                dve.wait_ge(vec, linked[0])

            def masked(h, i, at):
                hb, ahead = before(h, at)
                if i < 6:
                    old = i if i < 4 else i + 2
                    row_free = N.value("t", (hb, old, len(parts(old)) - 1), at, ahead)
                else:
                    row_free = N.value("t", (h, i - 2, 1), at)
                need_apart(dve, dve_passed, (s_full, N.value("s", (h, i), at)), (t_full, row_free))
                n, c0 = P * (i + 1), score_at(i)
                nc.vector.tensor_tensor_reduce(row(i), S_flat[:, c0:c0 + n], mask[:, T - n:T], -SCALE, 3.4e38,
                                               ALU.add, ALU.min, negmax[:, i:i + 1]).then_inc(s_masked, 1)

            def inverse(h, i, at):
                need(dve, s_exp, N.value("s", (h, i), at))
                nc.vector.reciprocal(rowinv[:, i:i + 1], rowsum[:, i:i + 1]).then_inc(s_inv, 1)

            def transposed_lo(h, i, at, ahead=0):
                for part, js in enumerate(parts(i)):
                    name = (h, i, part)
                    need(dve, t_hi, N.value("t", name, at, ahead))
                    src = TB[:, N.slot("t", name, at, ahead), 0:len(js) * P].rearrange("p (a b) -> p a b", b=P)
                    nc.vector.tensor_tensor(pt_of(i, part, False), src, f32(pt_of(i, part, True)),
                                            ALU.subtract).then_inc(t_lo, 1)

            def value_lo(half, at):
                name = ("v", half)
                need(dve, t_hi, N.value("t", name, at))
                src = TB[:, N.slot("t", name, at), :].rearrange("p (a b) -> p a b", b=P)
                rows = slice(4 * half, 4 * half + 4)
                nc.vector.tensor_tensor(v_lo[:, rows, :], src, f32(v_hi[:, rows, :]), ALU.subtract).then_inc(t_lo, 1)

            def output_lo(h, half, at, ahead=0):
                name = (("pva", "pvb")[half], h)
                n = 2 * h + half + 1
                n = n + 2 * R * (at.g + ahead) if at.turn is None else n + 2 * R * (at.g + ahead) + at.turn * (2 * R)
                dve.wait_ge(a_hi, n)
                cols = slice(half * HALF, (half + 1) * HALF)
                nc.vector.tensor_tensor(o_lo[:, h, cols], ACC[:, N.slot("a", name, at, ahead), :],
                                        f32(o_hi[:, h, cols]), ALU.subtract).then_inc(a_taken, 1)

            def times_cos(name, at, ahead=0):
                kind, which = name
                half = which[1] if kind == "q" else which
                need(dve, a_swapped, N.value("r", name, at, ahead))
                need(dve, r_lo, back_of(N.value("r", name, at, ahead), 2))
                nc.vector.tensor_tensor(qc[:, N.slot("r", name, at, ahead), :], ACC[:, N.slot("a", name, at, ahead), :],
                                        trig[:, 0, half * HALF:(half + 1) * HALF], ALU.mult).then_inc(a_taken, 1)

            def rotated_lo(name, at, ahead=0):
                kind, which = name
                half = which[1] if kind == "q" else which
                cols = slice(half * HALF, (half + 1) * HALF)
                hi, lo = (q_hi, q_lo) if kind == "q" else (k_hi, k_lo)
                need(dve, r_hi, N.value("r", name, at, ahead))
                nc.vector.tensor_tensor(lo[:, cols], qc[:, N.slot("r", name, at, ahead), :], f32(hi[:, cols]),
                                        ALU.subtract).then_inc(r_lo, 1)

            def copy_values(half, at, ahead=0):
                name = ("v", half)
                need(dve, a_full, N.value("a", name, at, ahead))
                need(dve, t_full, N.value("t", name, at, ahead - 1))
                nc.vector.tensor_copy(vt[:, half * HALF:(half + 1) * HALF],
                                      ACC[:, N.slot("a", name, at, ahead), :]).then_inc(a_taken, 1)

            def add_output(t, at, ahead):
                name = ("wo", t)
                need(dve, a_full, N.value("a", name, at, ahead))
                dve.wait_ge(y_zero, 1)
                need(dve, a_taken, back_of(N.value("a", name, at, ahead), 2))
                nc.vector.tensor_tensor(y[:, t, :], ACC[:, N.slot("a", name, at, ahead), :], y[:, t, :],
                                        ALU.add).then_inc(a_taken, 1)

            def split_lo(what, at, ahead=0):
                kind, r = what
                s = w_slot(what, at, ahead)
                dve.wait_ge(w_hi, w_number(what, at, ahead))
                hi, lo = {"q": (wq_hi, wq_lo), "k": (wk_hi, wk_lo), "v": (wv_hi, wv_lo), "wo": (wo_hi, wo_lo)}[kind]
                if kind == "wo":
                    hi, lo = hi[:, r, :], lo[:, r, :]
                else:
                    hi, lo = hi[:].rearrange("p k n -> p (k n)"), lo[:].rearrange("p k n -> p (k n)")
                nc.vector.tensor_tensor(lo, stage[:, s, :], f32(hi), ALU.subtract).then_inc(w_lo, 1)

            def take_modulation(m, at):
                name = ("mod", m)
                dve.wait_ge(a_full, N.value("a", name, at))
                acc = ACC[:, N.slot("a", name, at), :]
                if m < 2:
                    nc.vector.tensor_copy(modc[:, 2 * m, :], acc[:, 0:KC])
                    link(nc.vector.tensor_scalar(modc[:, 2 * m + 1, :], acc[:, KC:2 * KC], 1.0, None, ALU.add))
                    nc.vector.engine_nop().then_inc(a_taken, 1)
                else:
                    gate = (ga_b, gb_b)[m - 2]
                    link(nc.vector.tensor_scalar(gate[:], acc, 0.0, 2.0, ALU.is_ge, ALU.mult))
                    link(nc.vector.scalar_tensor_tensor(out=acc, in0=gate[:], scalar=-1.0, in1=acc, op0=ALU.add,
                                                        op1=ALU.mult))
                    link(nc.vector.tensor_scalar(acc, acc, 0.25, None, ALU.max))
                    nc.vector.scalar_tensor_tensor(out=gate[:], in0=gate[:], scalar=-1.0, in1=acc, op0=ALU.add,
                                                   op1=ALU.mult).then_inc(a_taken, 1)

            def fill(h, place, at, jobs=slice(None), back=0):
                for what, which, ahead in fillers(h, place, at.g == back)[jobs]:
                    ahead -= back
                    if what in "qk":
                        times_cos((what, which), at, ahead)
                    elif what == "v":
                        copy_values(which, at, ahead)
                    elif what == "wo":
                        add_output(which, at, ahead)
                    else:
                        if which == 2:
                            dve.wait_ge(t_full, N.value("t", ("v", 1), at))
                            dve.wait_ge(tab_in, 32)
                            for k in range(KC):
                                ins = nc.vector.tensor_scalar(vt[:, k * P:(k + 1) * P], mask[:, 0:P],
                                                              silu[:, 3, k:k + 1], None, ALU.add)
                            ins.then_inc(silu_done, 1)
                        take_modulation(which, at)

            def front(h, at):
                hb, ahead = before(h, at)
                masked(h, 0, at)
                masked(h, 1, at)
                if h or not at.first:
                    fill(hb, 5, at, slice(-1, None), -ahead)
                inverse(h, 0, at)
                inverse(h, 1, at)
                fill(h, 1, at)
                masked(h, 2, at)
                if h or not at.first:
                    transposed_lo(hb, 7, at, ahead)
                masked(h, 3, at)
                inverse(h, 2, at)
                inverse(h, 3, at)
                if h or not at.first:
                    rotated_lo(("q", (h, 1)), at)
                if h == 0:
                    rotated_lo(("k", 1), at)
                if h < R - 1:
                    split_lo(("q", h + 1), at)
                else:
                    split_lo(("wo", 3), at)
                if h or not at.first:
                    output_lo(hb, 1, at, ahead)
                if h == 0:
                    value_lo(0, at)
                    value_lo(1, at)

            def back(h, at):
                last = h == R - 1
                masked(h, 4, at)
                fill(h, 2, at)
                transposed_lo(h, 0, at)
                transposed_lo(h, 1, at)
                if last:
                    split_lo(("q", 0), at, 1)
                masked(h, 5, at)
                inverse(h, 4, at)
                fill(h, 3, at)
                transposed_lo(h, 2, at)
                transposed_lo(h, 3, at)
                inverse(h, 5, at)
                if h == 1:
                    split_lo(("wo", 0), at)
                if h == 2:
                    split_lo(("wo", 1), at)
                fill(h, 4, at, slice(0, -1))
                transposed_lo(h, 4, at)
                masked(h, 6, at)
                fill(h, 4, at, slice(-1, None))
                if last:
                    split_lo(("k", 0), at, 1)
                inverse(h, 6, at)
                output_lo(h, 0, at)
                transposed_lo(h, 5, at)
                masked(h, 7, at)
                rotated_lo(("q", ((h + 1) % R, 0)), at, int(last))
                inverse(h, 7, at)
                if h == 2:
                    split_lo(("wo", 2), at)
                if last:
                    split_lo(("v", 0), at, 1)
                fill(h, 5, at, slice(0, -1))
                if last:
                    rotated_lo(("k", 0), at, 1)
                transposed_lo(h, 6, at)

            for half in range(2):
                for t in range(4 * half, 4 * half + 4):
                    dve.wait_ge(x_in[t], 16)
                    link(nc.vector.bn_stats(stats[:, t, :], x_tile(t)))
                    link(nc.vector.bn_aggr(mv[:, t, :], stats[:, t, :]))
                nc.vector.tensor_scalar(rstd[:, 4 * half:4 * half + 4], mv[:, 4 * half:4 * half + 4, 1], EPS, None,
                                        ALU.add).then_inc(ln_stat, 1)
                dve.wait_ge(ln_std, half + 1)
                link(nc.vector.reciprocal(rstd[:, 4 * half:4 * half + 4], rstd[:, 4 * half:4 * half + 4]))
                for t in range(4 * half, 4 * half + 4):
                    nc.vector.tensor_scalar(x_tile(t), x_tile(t), mv[:, t, 0:1], rstd[:, t:t + 1], ALU.subtract,
                                            ALU.mult).then_inc(xn_done, 1)
            dve.wait_ge(silu_done_exp, 1)
            link(nc.vector.tensor_scalar(silu[:, 1, :], silu[:, 1, :], 1.0, None, ALU.add))
            link(nc.vector.reciprocal(silu[:, 2, :], silu[:, 1, :]))
            nc.vector.tensor_tensor(silu[:, 3, :], silu[:, 0, :], silu[:, 2, :], ALU.mult).then_inc(silu_done, 1)
            g0 = Group(0)
            for what in W_FIRST[:2]:
                split_lo(what, g0)
            take_modulation(0, g0)

            def h_rest(n):
                half, k = divmod(n, KC)
                cols = slice(half * HALF, (half + 1) * HALF)
                dve.wait_ge(h_hi_done, n + 1)
                nc.vector.tensor_tensor(h_lo[:, k, cols], vt[:, (n % 2) * HALF:(n % 2 + 1) * HALF],
                                        f32(h_hi[:, k, cols]), ALU.subtract).then_inc(h_done, 1)

            for n in range(2 * KC):
                half, k = divmod(n, KC)
                dve.wait_ge(xt_full, n + 1)
                if n >= 2:
                    dve.wait_ge(h_done, n - 1)
                nc.vector.tensor_scalar(vt[:, (n % 2) * HALF:(n % 2 + 1) * HALF], S[:, k, :], modc[:, 1, k:k + 1],
                                        modc[:, 0, k:k + 1], ALU.mult, ALU.add).then_inc(h_f32, 1)
                if n >= 1:
                    h_rest(n - 1)
            h_rest(2 * KC - 1)
            dve.wait_ge(tab_in, 32)
            times_cos(("k", 0), g0)
            times_cos(("q", (0, 0)), g0)
            rotated_lo(("k", 0), g0)
            split_lo(W_FIRST[2], g0)
            rotated_lo(("q", (0, 0)), g0)
            times_cos(("q", (0, 1)), g0)
            rotated_lo(("q", (0, 1)), g0)
            copy_values(0, g0)
            copy_values(1, g0)
            for h in range(R - 1):
                front(h, g0)
                back(h, g0)
            front(R - 1, g0)
            with dve.Fori(0, GROUPS - 1) as turn:
                at = Group(1, turn)
                back(R - 1, Group(0, turn))
                for h in range(R - 1):
                    front(h, at)
                    back(h, at)
                front(R - 1, at)

            def weight_lo(name, hi, lo, rows=P):
                dve.wait_ge(t_hi, N.value("t", name, G7))
                nc.vector.tensor_tensor(lo, TB[0:rows, N.slot("t", name, G7), :], f32(hi), ALU.subtract).then_inc(t_lo, 1)

            masked(3, 4, G7)
            weight_lo(("W", 0), fw_hi[:, 0, :], fw_lo[:, 0, :])
            weight_lo(("W", 1), fw_hi[:, 1, :], fw_lo[:, 1, :])
            transposed_lo(3, 0, G7)
            transposed_lo(3, 1, G7)
            masked(3, 5, G7)
            inverse(3, 4, G7)
            weight_lo(("W", 2), fw_hi[:, 2, :], fw_lo[:, 2, :])
            weight_lo(("W", 3), fw_hi[:, 3, :], fw_lo[:, 3, :])
            transposed_lo(3, 2, G7)
            transposed_lo(3, 3, G7)
            inverse(3, 5, G7)
            dve.wait_ge(t_hi, N.value("t", ("A", 0), G7))
            nc.vector.engine_nop().then_inc(t_lo, 1)
            weight_lo(("B", 0), fb_hi, fb_lo, MAX_R)
            transposed_lo(3, 4, G7)
            masked(3, 6, G7)
            inverse(3, 6, G7)
            output_lo(3, 0, G7)
            transposed_lo(3, 5, G7)
            masked(3, 7, G7)
            add_output(0, G7, 0)
            inverse(3, 7, G7)
            add_output(1, G7, 0)
            transposed_lo(3, 6, G7)
            add_output(2, G7, 0)
            add_output(3, G7, 0)
            transposed_lo(3, 7, G7)
            output_lo(3, 1, G7)
            for t in range(NT // 2, NT):
                add_output(t, G7, 0)

            def second_norm(t):
                s = t % 2
                dve.wait_ge(f_x2, t + 1)
                link(nc.vector.bn_stats(stats[:, t, :], y[:, t, :]))
                link(nc.vector.bn_aggr(mv[:, t, :], stats[:, t, :]))
                nc.vector.tensor_scalar(rstd[:, t:t + 1], mv[:, t, 1:2], EPS, None, ALU.add).then_inc(f_stat, 1)
                dve.wait_ge(f_std, t + 1)
                link(nc.vector.reciprocal(rstd[:, t:t + 1], rstd[:, t:t + 1]))
                if t >= 2:
                    dve.wait_ge(f_tr, t - 1)
                else:
                    dve.wait_ge(t_full, N.value("t", (3, 3, 0), G7))
                nc.vector.tensor_scalar(xn2(s), y[:, t, :], mv[:, t, 0:1], rstd[:, t:t + 1], ALU.subtract,
                                        ALU.mult).then_inc(f_xn, 1)

            def second_h(t):
                s = t % 2
                dve.wait_ge(f_aff, 2 * (t + 1))
                for k in range(KC // 2, KC):
                    ins = nc.vector.tensor_scalar(h2_f(s)[:, k * P:(k + 1) * P], S[:, 2 + s, k * P:(k + 1) * P],
                                                  modc[:, 3, k:k + 1], modc[:, 2, k:k + 1], ALU.mult, ALU.add)
                ins.then_inc(f_affv, 1)
                dve.wait_ge(f_hi, t + 1)
                nc.vector.tensor_tensor(h2_lo(s).rearrange("p k n -> p (k n)"), h2_f(s),
                                        f32(h2_hi(s).rearrange("p k n -> p (k n)")), ALU.subtract).then_inc(f_lo, 1)

            def route(t):
                s = t % 2
                g = lambda n, a=0, b=NR: gs[:, s, n, a:b]
                dve.wait_ge(f_gate, t + 1)
                if t == 0:
                    dve.wait_ge(b_in, 32)
                link(nc.vector.tensor_tensor(g(0), TB[:, s, MAX_R:AG], gate_bb[:], ALU.add))
                link(nc.vector.reduce_max(g(1, 0, 1), g(0), AX_X))
                nc.vector.tensor_scalar(g(1, 1, 2), g(1, 0, 1), -1.0, None, ALU.mult).then_inc(f_smax, 1)
                dve.wait_ge(f_exp, t + 1)
                link(nc.vector.reciprocal(g(1, 3, 4), g(1, 2, 3)))
                link(nc.vector.tensor_scalar(g(3), g(2), g(1, 3, 4), None, ALU.mult))
                link(nc.vector.reduce_max(g(4, 0, 1), g(3), AX_X))
                link(nc.vector.tensor_scalar(g(5), g(3), g(4, 0, 1), None, ALU.is_lt))
                nc.vector.reciprocal(g(4, 1, 2), g(4, 0, 1))
                link(nc.vector.tensor_tensor(g(6, 1, 2), g(5, 0, 1), g(5, 1, 2), ALU.mult))
                link(nc.vector.tensor_tensor(g(6, 2, 3), g(6, 1, 2), g(5, 2, 3), ALU.mult))
                link(nc.vector.tensor_tensor(g(4, 2, 3), g(4, 0, 1), g(4, 1, 2), ALU.mult))
                keep = [None, g(5, 0, 1), g(6, 1, 2), g(6, 2, 3)]
                for k in range(NR):
                    a = RANKS[k - 1] if k else 0
                    ins = nc.vector.tensor_scalar(tm(s)[:, a:RANKS[k]], TB[:, s, a:RANKS[k]], g(4, 2, 3), keep[k],
                                                  ALU.mult, *([ALU.mult] if k else []))
                ins.then_inc(f_tm, 1)

            def low_rank_lo(t):
                s = t % 2
                dve.wait_ge(f_tmhi, t + 1)
                nc.vector.tensor_tensor(tm_lo(s), TB[0:MAX_R, s, 2 * P:3 * P], f32(tm_hi(s)), ALU.subtract).then_inc(f_tmlo, 1)

            def result(t):
                s = t % 2
                dve.wait_ge(f_full, t + 1)
                nc.vector.tensor_tensor(f_tmp(s), S[:, s, :], ffn_bias, ALU.add).then_inc(f_sum, 1)
                dve.wait_ge(f_sum, t + 1)
                link(nc.vector.tensor_tensor(f_tmp(s), f_tmp(s), gb_b[:], ALU.mult))
                nc.vector.tensor_tensor(y[:, t, :], y[:, t, :], f_tmp(s), ALU.add).then_inc(f_out, 1)

            for t in range(NT + 1):
                if t < NT:
                    second_norm(t)
                    second_h(t)
                if t >= 1:
                    low_rank_lo(t - 1)
                if t < NT:
                    route(t)
                if t >= 1:
                    result(t - 1)

        @block.gpsimd
        def _(pool):
            def normalise(h, i, at):
                need_apart(pool, pool_passed, (s_inv, N.value("s", (h, i), at)))
                nc.gpsimd.tensor_scalar(row(i), row(i), rowinv[:, i:i + 1], 1.0, ALU.mult, ALU.mult).then_inc(s_norm, 1)

            def rotate(name, at, ahead=0):
                kind, which = name
                half = which[1] if kind == "q" else which
                s = N.slot("r", name, at, ahead)
                n = N.value("r", name, at, ahead)
                need(pool, a_swapped, n)
                nc.gpsimd.tensor_tensor(qr[:, s, :], qr[:, s, :], trig[:, 1, half * HALF:(half + 1) * HALF],
                                        ALU.mult).then_inc(r_sin, 1)
                need(pool, r_sin, n)
                need(pool, a_taken, N.value("a", name, at, ahead))
                nc.gpsimd.tensor_tensor(qc[:, s, :], qc[:, s, :], qr[:, s, :], ALU.add).then_inc(r_sum, 1)

            def front(h, at):
                if h or not at.first:
                    rotate(("q", (h, 1)), at)
                normalise(h, 0, at)
                normalise(h, 1, at)
                if h == 0:
                    rotate(("k", 1), at)
                normalise(h, 2, at)
                normalise(h, 3, at)

            def back(h, at):
                last = h == R - 1
                normalise(h, 4, at)
                normalise(h, 5, at)
                rotate(("q", ((h + 1) % R, 0)), at, int(last))
                normalise(h, 6, at)
                normalise(h, 7, at)
                if last:
                    rotate(("k", 0), at, 1)

            for buf, tile in ((pa_hi, 11), (pa_lo, 11), (pb_hi, 27), (pb_lo, 27)):
                ins = nc.gpsimd.memset(f32(buf[:, tile, :]), 0.0)
            ins.then_inc(zeroed, 1)
            g0 = Group(0)
            pool.wait_ge(tab_in, 32)
            rotate(("k", 0), g0)
            rotate(("q", (0, 0)), g0)
            rotate(("q", (0, 1)), g0)
            for h in range(R - 1):
                front(h, g0)
                if h == 1:
                    pool.wait_ge(a_full, N.value("a", ("mod", 3), g0))
                    nc.gpsimd.memset(y[:], 0.0).then_inc(y_zero, 1)
                back(h, g0)
            front(R - 1, g0)
            with pool.Fori(0, GROUPS - 1) as turn:
                at = Group(1, turn)
                back(R - 1, Group(0, turn))
                for h in range(R - 1):
                    front(h, at)
                    back(h, at)
                front(R - 1, at)
            for i in range(4, 8):
                normalise(3, i, G7)
            for t in range(NT):
                pool.wait_ge(a_taken, N.value("a", ("wo", t), G7))
                nc.gpsimd.tensor_tensor(y[:, t, :], y[:, t, :], ga_b[:], ALU.mult).then_inc(f_ga, 1)
                pool.wait_ge(f_ga, t + 1)
                pool.wait_ge(f_x[t % 4], 16 * (t // 4 + 1))
                nc.gpsimd.tensor_tensor(y[:, t, :], y[:, t, :], x_again(t), ALU.add).then_inc(f_x2, 1)
    return nc


_INS = ["L0_attn_x", "L0_attn_wq", "L0_attn_wk", "L0_attn_wv", "L0_attn_wo", "L0_ffn_W", "L0_ffn_b", "L0_ffn_A",
        "L0_ffn_B", "L0_ffn_gate_w", "L0_ffn_gate_b", "L0_c", "L0_wmod"]
_OUTS = [((1, T, D), "float32")]


def kernel(**inputs):
    import numpy as _np
    import concourse.bacc as _bacc
    from concourse import mybir as _mybir
    from concourse.bass_utils import run_bass_kernel_spmd as _run

    nc = _bacc.Bacc("TRN2", target_bir_lowering=False, num_devices=1, dynamic_dma_scratch_size=1024)
    arrays, args = {}, []
    for name in _INS:
        a = _np.ascontiguousarray(inputs[name])
        arrays[f"in_{name}_dram"] = a
        args.append(nc.dram_tensor(f"in_{name}_dram", a.shape, _mybir.dt.from_np(a.dtype), kind="ExternalInput").ap())
    for i, (shape, dtype) in enumerate(_OUTS):
        dt = _mybir.dt.from_np(_np.dtype(dtype))
        args.append(nc.dram_tensor(f"out_{i}_dram", shape, dt, kind="ExternalOutput").ap())
    adaln_block(nc, *args)
    r = _run(nc, [arrays], core_ids=[0])
    got = tuple(r.results[0][f"out_{i}_dram"] for i in range(len(_OUTS)))
    return got[0]
```

```python
from contextlib import ExitStack

import numpy as np

import concourse.bass as bass
from concourse import mybir
from concourse.alu_op_type import AluOpType as ALU

ACT = mybir.ActivationFunctionType
AX_X = mybir.AxisListType.X
F32 = mybir.dt.float32
F32R = mybir.dt.float32r

P = 128
T = 1024
NT = T // P
D = 512
KC = D // P
HEADS, KV_HEADS, HD = 32, 8, 128
GROUPS = KV_HEADS
R = HEADS // KV_HEADS
HALF = 512
SCALE = 1.0 / float(np.sqrt(HD))
EPS = 1e-5
MASKED = -3.0e38
RANKS = (8, 16, 32, 64)
NR = len(RANKS)
MAX_R = RANKS[-1]
AG = MAX_R + NR


def rope_tables():
    theta, factor, hi_ff, lo_ff, orig = 500000.0, 8.0, 4.0, 1.0, 1024
    inv = 1.0 / theta ** (np.arange(0, HD, 2, dtype=np.float64) / HD)
    wavelen = 2.0 * np.pi / inv
    low_wl, high_wl = orig / lo_ff, orig / hi_ff
    smooth = (orig / wavelen - lo_ff) / (hi_ff - lo_ff)
    scaled = np.where(wavelen > low_wl, inv / factor, inv)
    mid = (wavelen <= low_wl) & (wavelen >= high_wl)
    scaled = np.where(mid, (1 - smooth) * inv / factor + smooth * inv, scaled).astype(np.float32)
    freqs = np.arange(T, dtype=np.float32)[:, None] * scaled[None, :]
    emb = np.concatenate([freqs, freqs], axis=-1)
    cos, sin = np.cos(emb).astype(np.float32).T, np.sin(emb).astype(np.float32).T
    sign = np.where(np.arange(HD) < HD // 2, -1.0, 1.0).astype(np.float32)[:, None]
    return np.ascontiguousarray(np.stack([cos, sin * sign], axis=1))


def causal_mask():
    m = np.zeros((P, T), np.float32)
    m[:, T - P:] = np.where(np.arange(P)[None, :] > np.arange(P)[:, None], MASKED, 0.0)
    return m


def rank_columns():
    return np.tile(np.concatenate([RANKS, np.arange(MAX_R), [-0.5]]).astype(np.float32), (P, 1))


def fillers(h, place, first):
    wo = lambda *tiles: [] if first else [("wo", t, -1) for t in tiles]
    mod = lambda *which: [("mod", m, 0) for m in which] if first else []
    jobs = {
        (0, 1): [] if first else [("k", 1, 0)],
        (0, 2): wo(0) + mod("sb"),
        (0, 3): wo(1) + mod("cb"),
        (0, 4): wo(2, 3) + mod("second") + [("q", (1, 0), 0)],
        (0, 5): wo(4, 5, 6) + mod("ga", "gb") + [("q", (1, 1), 0)],
        (1, 1): wo(7),
        (1, 4): [("q", (2, 0), 0)],
        (1, 5): [("q", (2, 1), 0)],
        (2, 4): [("q", (3, 0), 0)],
        (2, 5): [("q", (3, 1), 0)],
        (3, 4): [("q", (0, 0), 1)],
        (3, 5): [("k", 0, 1), ("q", (0, 1), 1), ("v", 0, 1), ("v", 1, 1)],
    }
    return jobs.get((h, place), [])


def parts(i):
    return [range(0, min(i, 3) + 1)] + ([range(4, i + 1)] if i >= 4 else [])


class Numbers:

    def __init__(self):
        self.count = dict.fromkeys("star", 0)
        self.of = {}
        for job in (("mod", "sa", 0), ("mod", "ca", 0), ("mod", "first", 0), ("k", 0, 0), ("q", (0, 0), 0), ("q", (0, 1), 0), ("k", 1, 0), ("v", 0, 0),
                    ("v", 1, 0)):
            self.job(job, 0)
        marks = []
        for g in range(GROUPS):
            if g:
                self.back(3, g - 1, first=False)
            for h in range(R):
                self.front(h, g, first=g == 0)
                if h < R - 1:
                    self.back(h, g, first=g == 0)
            marks.append(dict(self.count))
        self.per = {k: marks[2][k] - marks[1][k] for k in "star"}
        assert all(v % 2 == 0 for v in self.per.values())
        self.tail()

    def step(self, kind, name, g):
        self.count[kind] += 1
        self.of[kind, name, g] = self.count[kind]

    def job(self, job, g):
        what, which, ahead = job
        self.step("a", (what, which), g + ahead)
        if what in "qk":
            self.step("r", (what, which), g + ahead)

    def banks(self, h, i, g):
        for part in range(len(parts(i))):
            self.step("t", (h, i, part), g)

    def front(self, h, g, first):
        before = (h - 1, g) if h else (R - 1, g - 1)
        self.step("s", (h, 0), g)
        self.step("s", (h, 1), g)
        for job in fillers(h, 1, first):
            self.job(job, g)
        self.step("s", (h, 2), g)
        if before[1] >= 0:
            self.banks(before[0], 7, before[1])
        self.step("s", (h, 3), g)
        if before[1] >= 0:
            self.job(("pvb", before[0], 0), before[1])
        if h == 0:
            self.step("t", ("v", 0), g)
            self.step("t", ("v", 1), g)

    def back(self, h, g, first, jobs=fillers):
        self.step("s", (h, 4), g)
        for job in jobs(h, 2, first):
            self.job(job, g)
        self.banks(h, 0, g)
        self.banks(h, 1, g)
        self.step("s", (h, 5), g)
        for job in jobs(h, 3, first):
            self.job(job, g)
        self.banks(h, 2, g)
        self.banks(h, 3, g)
        for job in jobs(h, 4, first):
            self.job(job, g)
        self.banks(h, 4, g)
        self.step("s", (h, 6), g)
        self.job(("pva", h, 0), g)
        self.banks(h, 5, g)
        self.step("s", (h, 7), g)
        for job in jobs(h, 5, first):
            self.job(job, g)
        self.banks(h, 6, g)

    def tail(self):
        g = GROUPS - 1
        self.step("s", (3, 4), g)
        self.banks(3, 0, g)
        self.banks(3, 1, g)
        self.step("s", (3, 5), g)
        self.job(("W", 0, 0), g)
        self.banks(3, 2, g)
        self.banks(3, 3, g)
        self.job(("W", 1, 0), g)
        self.job(("pva", 3, 0), g)
        self.banks(3, 4, g)
        self.step("s", (3, 6), g)
        self.job(("W", 2, 0), g)
        self.banks(3, 5, g)
        self.job(("W", 3, 0), g)
        self.step("s", (3, 7), g)
        self.job(("A", 0, 0), g)
        self.job(("wo", 0, 0), g)
        self.job(("B", 0, 0), g)
        self.banks(3, 6, g)
        self.job(("wo", 1, 0), g)
        self.banks(3, 7, g)
        self.job(("wo", 2, 0), g)
        self.job(("pvb", 3, 0), g)
        for t in range(3, NT):
            self.job(("wo", t, 0), g)

    def value(self, kind, name, at, ahead=0):
        if at.turn is None:
            return self.of.get((kind, name, at.g + ahead))
        base = self.of[kind, name, at.g + ahead]
        for turn in range(GROUPS - 1):
            assert self.of[kind, name, at.g + ahead + turn] == base + self.per[kind] * turn
        return base + at.turn * self.per[kind]

    def slot(self, kind, name, at, ahead=0):
        return (self.of[kind, name, at.g + ahead] - 1) % 2


    def last(self, kind, at, *steps):
        def base(step):
            return self.of.get((kind, step[0], at.g + step[1]), -9) - step[2]
        name, ahead, less = max(steps, key=base)
        return back_of(self.value(kind, name, at, ahead), less)


class Group:

    def __init__(self, g, turn=None):
        self.g, self.turn = g, turn

    @property
    def index(self):
        return self.g if self.turn is None else self.g + self.turn

    @property
    def first(self):
        return self.g == 0


def back_of(n, k):
    if n is None or k == 0:
        return n
    if isinstance(n, int):
        return n - k if n > k else None
    return n - k


def need(engine, semaphore, value):
    if value is not None:
        engine.wait_ge(semaphore, value)


def need_apart(engine, passed, *waits):
    for semaphore, n in waits:
        need(engine, semaphore, n)
    engine.sem_inc(passed, 1)


def adaln_block(nc, x, wq, wk, wv, wo, ffn_w, ffn_b, ffn_a, ffn_bb, gate_w, gate_b, c, wmod, out):
    N = Numbers()
    trig_c = nc.inline_tensor(rope_tables(), name="rope_tables").ap()
    mask_c = nc.inline_tensor(causal_mask(), name="causal_mask").ap()
    ranks_c = nc.inline_tensor(rank_columns(), name="rank_columns").ap()
    ident_c = nc.inline_tensor(np.eye(P, dtype=np.float32), name="identity").ap()

    with ExitStack() as ctx:
        sb = lambda name, shape, dt=F32: ctx.enter_context(nc.sbuf_tensor(name, shape, dt))
        sem = lambda name: ctx.enter_context(nc.semaphore(name))

        h_hi, h_lo = sb("h_hi", [P, KC, T], F32R), sb("h_lo", [P, KC, T], F32R)
        k_hi, k_lo = sb("k_hi", [P, T], F32R), sb("k_lo", [P, T], F32R)
        q_hi, q_lo = sb("q_hi", [P, T], F32R), sb("q_lo", [P, T], F32R)
        v_hi, v_lo = sb("v_hi", [P, NT, HD], F32R), sb("v_lo", [P, NT, HD], F32R)
        pa_hi, pa_lo = sb("pa_hi", [P, 13, P], F32R), sb("pa_lo", [P, 13, P], F32R)
        pb_hi, pb_lo = sb("pb_hi", [P, 29, P], F32R), sb("pb_lo", [P, 29, P], F32R)
        o_hi, o_lo = sb("o_hi", [P, R, T], F32R), sb("o_lo", [P, R, T], F32R)
        wq_hi, wq_lo = sb("wq_hi", [P, KC, HD], F32R), sb("wq_lo", [P, KC, HD], F32R)
        wk_hi, wk_lo = sb("wk_hi", [P, KC, HD], F32R), sb("wk_lo", [P, KC, HD], F32R)
        wv_hi, wv_lo = sb("wv_hi", [P, KC, HD], F32R), sb("wv_lo", [P, KC, HD], F32R)
        wo_hi, wo_lo = sb("wo_hi", [P, R, D], F32R), sb("wo_lo", [P, R, D], F32R)
        y = sb("y", [P, NT, D])
        trig = sb("trig", [P, 2, T])
        mask = sb("mask", [P, T])
        ident = sb("ident", [P, P])
        stage = sb("stage", [P, 2, D])
        qc = sb("qc", [P, 2, HALF])
        qr = sb("qr", [P, 2, HALF])
        vt = sb("vt", [P, T])
        p_small = sb("p_small", [P, 1280])
        p_large = sb("p_large", [P, 2, T])
        ga_b, gb_b = sb("ga_b", [P, D]), sb("gb_b", [P, D])
        silu = sb("silu", [P, 4, KC])
        modc = sb("modc", [P, 4, KC])
        negmax, rowsum, rowinv = sb("negmax", [P, NT]), sb("rowsum", [P, NT]), sb("rowinv", [P, NT])
        stats, mv = sb("stats", [P, NT, 6]), sb("mv", [P, NT, 2])
        rstd, shift = sb("rstd", [P, NT]), sb("shift", [P, NT])
        ranks = sb("ranks", [P, NR + MAX_R + 1])
        gate_bb = sb("gate_bb", [P, NR])
        gs = sb("gs", [P, 2, 7, NR])

        S = ctx.enter_context(nc.psum_tensor("scores", [P, 4, HALF], F32))
        TB = ctx.enter_context(nc.psum_tensor("transposed", [P, 2, HALF], F32))
        ACC = ctx.enter_context(nc.psum_tensor("accumulators", [P, 2, HALF], F32))
        S_flat = S[:].rearrange("p b n -> p (b n)")

        c_in, ident_in, tab_in = sem("c_in"), sem("ident_in"), sem("tab_in")
        x_in = [sem(f"x_in{t}") for t in range(NT)]
        mod_in = [sem(f"mod_in{k}") for k in range(KC)]
        stage_in = [sem("stage_in0"), sem("stage_in1")]
        silu_done_exp, silu_done, y_in = sem("silu_done_exp"), sem("silu_done"), sem("y_in")
        ln_var, ln_stat, xn_done, ranks_in = (sem(n) for n in ("ln_var", "ln_stat", "xn_done", "ranks_in"))
        root = sem("root")
        xt_full, h_f32, h_hi_done, h_done = sem("xt_full"), sem("h_f32"), sem("h_hi_done"), sem("h_done")
        s_full, s_masked, s_exp, s_inv, s_norm = (sem(n) for n in ("s_full", "s_masked", "s_exp", "s_inv", "s_norm"))
        t_full, t_hi, t_lo = sem("t_full"), sem("t_hi"), sem("t_lo")
        a_full, a_hi, a_swapped, a_taken = sem("a_full"), sem("a_hi"), sem("a_swapped"), sem("a_taken")
        r_sin, r_sum, r_hi, r_lo = sem("r_sin"), sem("r_sum"), sem("r_hi"), sem("r_lo")
        w_hi, w_lo, wo_scaled = sem("w_hi"), sem("w_lo"), sem("wo_scaled")
        vec = sem("vec")
        dve_passed, pool_passed = sem("dve_passed"), sem("pool_passed")
        f_in, f_low_in, f_var, f_stat, f_xn = (sem(n) for n in ("f_in", "f_low_in", "f_var", "f_stat", "f_xn"))
        f_whi = sem("f_whi")
        f_tr, f_aff, f_hi, f_lo = (sem(n) for n in ("f_tr", "f_aff", "f_hi", "f_lo"))
        f_gate, f_ffn, f_smax, f_exp, f_tm = (sem(n) for n in ("f_gate", "f_ffn", "f_smax", "f_exp", "f_tm"))
        f_tmt, f_tmhi, f_tmlo, f_full = (sem(n) for n in ("f_tmt", "f_tmhi", "f_tmlo", "f_full"))
        f_gated, f_bias, f_y, f_out, stored = (sem(n) for n in ("f_gated", "f_bias", "f_y", "f_out", "stored"))
        b_in = sem("b_in")

        def row(i, n=None):
            n = n or P * (i + 1)
            if i < 4:
                at = (0, 128, 384, 768)[i]
                return p_small[:, at:at + n]
            return p_large[:, i % 2, 0:n]

        def score_at(i):
            if i < 4:
                return HALF * i
            return (0, 2 * HALF)[i % 2] + (P if i == 4 else 0)

        PIECES = {0: [256], 1: [256], 2: [384], 3: [512], 4: [384, 256], 5: [512, 256], 6: [512, 384], 7: [512, 512]}
        SCORES_BEFORE = {0: (1, 6), 1: (1, 6), 2: (1, 7), 3: (1, 7), 4: (0, 1), 5: (0, 3), 6: (0, 4), 7: (0, 5)}

        def pt_of(i, part, hi):
            js = parts(i)[part]
            n = len(js)
            if i < 4:
                buf = pa_hi if hi else pa_lo
                return buf[:, i:i + 3 * (n - 1) + 1:3, :]
            buf = pb_hi if hi else pb_lo
            if part == 0:
                return buf[:, i - 4:i - 4 + 4 * (n - 1) + 1:4, :]
            at = 16 + i - 4
            return buf[:, at:at + 3 * (n - 1) + 1:3, :]

        def pt_row(j, half, hi):
            if half == 0:
                i0 = min(j, 2)
                buf, at = (pa_hi if hi else pa_lo), 3 * j + i0
                return i0 * P, buf[:, at:at + 4 - i0, :].rearrange("p a b -> p (a b)")
            buf = pb_hi if hi else pb_lo
            if j < 4:
                return 0, buf[:, 4 * j:4 * j + 4, :].rearrange("p a b -> p (a b)")
            i0 = min(j - 4, 2)
            at = 16 + 3 * (j - 4) + i0
            return i0 * P, buf[:, at:at + 4 - i0, :].rearrange("p a b -> p (a b)")

        def x_tile(t):
            return (qc, qr)[t // 2][:, t % 2, :] if t < 4 else p_large[:, (t - 4) // 2, (t % 2) * D:(t % 2 + 1) * D]

        def f32(ap):
            return ap.bitcast(F32)

        def before(h, at):
            return (h - 1, 0) if h else (R - 1, -1)

        W_FIRST = [("k", 0), ("q", 0), ("v", 0)]
        W_GROUP = [("q", 1), ("q", 2), ("wo", 0), ("q", 3), ("wo", 1), ("wo", 2), ("wo", 3)]
        W_NEXT = [("q", 0), ("k", 0), ("v", 0)]
        W_PER = len(W_GROUP) + len(W_NEXT)

        def w_number(what, at, ahead=0):
            if what in W_GROUP:
                base = len(W_FIRST) + W_GROUP.index(what) + 1 + W_PER * (at.g + ahead)
            elif at.g + ahead == 0:
                base = W_FIRST.index(what) + 1
            else:
                base = len(W_FIRST) + len(W_GROUP) + W_NEXT.index(what) + 1 + W_PER * (at.g + ahead - 1)
            return base if at.turn is None else base + at.turn * W_PER

        def w_slot(what, at, ahead=0):
            return (w_number(what, Group(at.g), ahead) - 1) % 2

        def stage_count(what, at, ahead=0):
            n = w_number(what, Group(at.g), ahead)
            value = 16 * ((n + 1) // 2)
            return value if at.turn is None else value + at.turn * (16 * W_PER // 2)

        y_flat = y[:].rearrange("p t n -> p (t n)")
        mod_w = y_flat.rearrange("p (k n) -> p k n", k=KC)

        fw_hi, fw_lo = h_hi[:, :, 0:D], h_lo[:, :, 0:D]
        h2_hi = lambda s: h_hi[:, s, D:T].rearrange("p (k n) -> p k n", k=KC)
        h2_lo = lambda s: h_lo[:, s, D:T].rearrange("p (k n) -> p k n", k=KC)
        fb_hi, fb_lo = h_hi[0:MAX_R, 2, D:T], h_lo[0:MAX_R, 2, D:T]
        tm_hi = lambda s: h_hi[0:MAX_R, 3, D + P * s:D + P * (s + 1)]
        tm_lo = lambda s: h_lo[0:MAX_R, 3, D + P * s:D + P * (s + 1)]
        fw_in = trig[:].rearrange("p a (b n) -> p (a b) n", b=2)
        ag_in = stage[0:AG, 0, :]
        fb_in = stage[:, 1, 0:KC * MAX_R].rearrange("p (k n) -> p k n", k=KC)
        ag_t = vt[:, 0:KC * AG].rearrange("p (k n) -> p k n", k=KC)
        tm = lambda s: vt[:, 512 + MAX_R * s:512 + MAX_R * (s + 1)]
        tm_f = lambda s: vt[:, 768 + MAX_R * s:768 + MAX_R * (s + 1)]
        xn2 = lambda s: p_small[:, D * s:D * (s + 1)]
        h2_f = lambda s: trig[:, s, 0:D]
        f_tmp = lambda s: trig[:, s, D:T]
        ffn_bias = mask[:, 0:D]

        G7 = Group(GROUPS - 1)
        block = ctx.enter_context(nc.Block())

        @block.sync
        def _(sp):
            x_v = x[0].rearrange("(t p) d -> t p d", p=P)
            wmod_v = wmod.rearrange("(k p) n -> p k n", p=P)
            sp.dma_start(silu[:, 0, :], c.rearrange("o (k p) -> p (o k)", p=P), allow_slow_non_contiguous=True).then_inc(c_in, 16)
            sp.dma_start(ranks[:], ranks_c).then_inc(ranks_in, 16)
            sp.dma_start(ident[:], ident_c).then_inc(ident_in, 16)
            for t in range(NT):
                if t < KC:
                    sp.dma_start(mod_w[:, t, :], wmod_v[:, t, 0:2 * D]).then_inc(mod_in[t], 16)
                sp.dma_start(x_tile(t), x_v[t]).then_inc(x_in[t], 16)

            weights = {"q": (wq, R), "k": (wk, 1), "v": (wv, 1)}

            def load(what, at, ahead=0):
                kind, r = what
                s = w_slot(what, at, ahead)
                need(sp, w_lo, back_of(w_number(what, at, ahead), 2))
                if kind == "wo":
                    src = wo[bass.ds(((at.index + ahead) * R + r) * HD, HD), :]
                    dst = stage[:, s, :]
                else:
                    w, per = weights[kind]
                    src = w.rearrange("(k p) n -> p k n", p=P)[:, :, bass.ds(((at.index + ahead) * per + r) * HD, HD)]
                    dst = stage[:, s, :].rearrange("p (k n) -> p k n", k=KC)
                sp.dma_start(dst, src).then_inc(stage_in[s], 16)

            g0 = Group(0)
            load(("k", 0), g0)
            load(("q", 0), g0)
            sp.dma_start(trig[:], trig_c).then_inc(tab_in, 16)
            load(("v", 0), g0)
            sp.dma_start(mask[:], mask_c).then_inc(tab_in, 16)
            sp.wait_ge(a_full, N.value("a", ("mod", "ca"), g0))
            sp.dma_start(mod_w, wmod_v[:, :, 3 * D:5 * D]).then_inc(mod_in[0], 16)
            load(("q", 1), g0)
            sp.wait_ge(a_full, N.value("a", ("mod", "sb"), g0))
            sp.dma_start(mod_w[:, :, 0:D], wmod_v[:, :, 2 * D:3 * D]).then_inc(mod_in[1], 16)
            sp.wait_ge(a_full, N.value("a", ("mod", "cb"), g0))
            sp.dma_start(mod_w[:, :, D:2 * D], wmod_v[:, :, 5 * D:6 * D]).then_inc(mod_in[2], 16)
            load(("q", 2), g0)
            load(("wo", 0), g0)
            sp.wait_ge(a_full, N.value("a", ("mod", "gb"), g0))
            sp.dma_start(y[:], x[0].rearrange("(t p) d -> p t d", p=P)).then_inc(y_in, 16)
            for what in W_GROUP[3:]:
                load(what, g0)
            with sp.Fori(0, GROUPS - 1) as turn:
                at = Group(1, turn)
                for what in W_NEXT:
                    load(what, at)
                for what in W_GROUP:
                    load(what, at)

            sp.wait_ge(r_sum, N.value("r", ("q", (3, 1)), G7))
            sp.wait_ge(a_taken, N.value("a", ("q", (3, 1)), G7))
            sp.dma_start(fw_in, ffn_w.rearrange("(o p) i -> p o i", p=P)).then_inc(f_in, 16)
            sp.wait_ge(w_lo, w_number(("wo", 3), G7))
            sp.dma_start(stage[0:MAX_R, 0, :], ffn_a).then_inc(f_low_in, 16)
            sp.dma_start(stage[MAX_R:AG, 0, :], gate_w).then_inc(f_low_in, 16)
            sp.dma_start(fb_in, ffn_bb.rearrange("(k p) r -> p k r", p=P)).then_inc(f_low_in, 16)
            sp.dma_start(gate_bb[:], gate_b.rearrange("(o r) -> o r", o=1).to_broadcast([P, NR])).then_inc(b_in, 16)
            sp.wait_ge(s_masked, N.value("s", (3, 7), G7))
            sp.dma_start(ffn_bias, ffn_b.rearrange("(o n) -> o n", o=1).to_broadcast([P, D])).then_inc(b_in, 16)
            for t in range(NT):
                sp.wait_ge(f_out, t + 1)
                sp.dma_start(out[0].rearrange("(t p) d -> t p d", p=P)[t], y[:, t, :]).then_inc(stored, 16)
            sp.wait_ge(stored, 16 * NT)

        @block.tensor
        def _(pe):
            def scores(h, i, at):
                back, tile = SCORES_BEFORE[i]
                hb, ahead = (h, 0) if not back else before(h, at)
                need(pe, s_masked, N.value("s", (hb, tile), at, ahead))
                half = i // 4
                need(pe, r_lo, N.last("r", at, (("q", (h, half)), 0, 0), (("k", half), 0, 0)))
                c0 = score_at(i)
                key = 0
                for n in PIECES[i]:
                    for k, (a, b) in enumerate(((q_hi, k_hi), (q_hi, k_lo), (q_lo, k_hi))):
                        mm = nc.tensor.matmul(S_flat[:, c0 + key:c0 + key + n], a[:, i * P:(i + 1) * P],
                                              b[:, key:key + n], start=(k == 0), stop=(k == 2))
                    key += n
                mm.then_inc(s_full, 1)

            def transposes(h, i, at, ahead=0):
                need(pe, s_norm, N.value("s", (h, i), at, ahead))
                for part, js in enumerate(parts(i)):
                    name = (h, i, part)
                    b = N.slot("t", name, at, ahead)
                    need(pe, t_lo, back_of(N.value("t", name, at, ahead), 2))
                    for j in js:
                        mm = nc.tensor.transpose(TB[:, b, (j % 4) * P:(j % 4 + 1) * P], row(i)[:, j * P:(j + 1) * P], ident[:])
                    mm.then_inc(t_full, 1)

            def bank_free(name, at, ahead):
                need(pe, a_taken, back_of(N.value("a", name, at, ahead), 2))

            def weighted(h, half, at, ahead=0):
                name = (("pva", "pvb")[half], h)
                bank_free(name, at, ahead)
                acc = ACC[:, N.slot("a", name, at, ahead), :]
                hi_lo = [(v_hi, True), (v_lo, True), (v_hi, False)]
                if half == 0:
                    steps = [(t_lo, (h, 3, 0), hi_lo, range(4))]
                else:
                    steps = [(t_hi, (h, 7, 0), hi_lo[:2], range(4)), (t_lo, (h, 7, 0), hi_lo[2:], range(4)),
                             (t_lo, (h, 7, 1), hi_lo, range(4, 8))]
                for done, tiles, products, keys in steps:
                    need(pe, done, N.value("t", tiles, at, ahead))
                    for v, hi in products:
                        for j in keys:
                            c0, pt = pt_row(j, half, hi)
                            mm = nc.tensor.matmul(acc[:, c0:HALF], v[:, j, :], pt, start=(hi and v is v_hi and j == 0),
                                                  stop=(not hi and j == 4 * half + 3))
                mm.then_inc(a_full, 1)

            def project(name, at, ahead=0):
                kind, which = name
                head, half = which if kind == "q" else (0, which)
                bank_free(name, at, ahead)
                pe.wait_ge(w_lo, w_number((kind, head), at, ahead))
                w, w_rest = {"q": (wq_hi, wq_lo), "k": (wk_hi, wk_lo), "v": (wv_hi, wv_lo)}[kind]
                acc = ACC[:, N.slot("a", name, at, ahead), :]
                n = 0
                for a, b in ((w, h_hi), (w, h_lo), (w_rest, h_hi)):
                    for k in range(KC):
                        mm = nc.tensor.matmul(acc, a[:, k, :], b[:, k, half * HALF:(half + 1) * HALF],
                                              start=(n == 0), stop=(n == 3 * KC - 1))
                        n += 1
                mm.then_inc(a_full, 1)

            def project_out(t, at, ahead):
                name = ("wo", t)
                need(pe, a_taken, N.last("a", at, (name, ahead, 2), ((("pva", "pvb")[t // 4], R - 1), ahead, 0)))
                pe.wait_ge(w_lo, w_number(("wo", R - 1), at, ahead))
                acc = ACC[:, N.slot("a", name, at, ahead), :]
                n = 0
                for a, b in ((o_hi, wo_hi), (o_hi, wo_lo), (o_lo, wo_hi)):
                    for r in range(R):
                        mm = nc.tensor.matmul(acc, a[:, r, t * P:(t + 1) * P], b[:, r, :],
                                              start=(n == 0), stop=(n == 3 * R - 1))
                        n += 1
                mm.then_inc(a_full, 1)

            def modulation(m, at):
                name = ("mod", m)
                bank_free(name, at, 0)
                acc = ACC[:, N.slot("a", name, at), :]
                if m in ("first", "second"):
                    pe.wait_ge(a_taken, N.value("a", name, at) - 1)
                    for n in range(2 * KC):
                        mm = nc.tensor.matmul(acc[:, n:n + 1], vt[0:1, n * P:(n + 1) * P], ident[0:1, 0:1],
                                              start=True, stop=True)
                else:
                    chunk, arrived = {"sb": (0, 0), "cb": (1, 0), "ga": (0, 1), "gb": (1, 2)}[m]
                    pe.wait_ge(mod_in[arrived], 32)
                    gate = m in ("ga", "gb")
                    if gate:
                        pe.wait_ge(silu_done, 2)
                    for k in range(KC):
                        mm = nc.tensor.matmul(acc if gate else acc[0:1, :],
                                              vt[:, k * P:(k + 1) * P] if gate else silu[:, 3, k:k + 1],
                                              mod_w[:, k, chunk * D:(chunk + 1) * D], start=(k == 0), stop=(k == KC - 1))
                mm.then_inc(a_full, 1)

            def value_transposes(half, at):
                name = ("v", half)
                b = N.slot("t", name, at)
                need(pe, t_lo, back_of(N.value("t", name, at), 2))
                need(pe, a_taken, N.value("a", ("v", half), at))
                for j in range(4):
                    c0 = half * HALF + j * P
                    mm = nc.tensor.transpose(TB[:, b, j * P:(j + 1) * P], vt[:, c0:c0 + P], ident[:])
                mm.then_inc(t_full, 1)

            def fill(h, place, at):
                for what, which, ahead in fillers(h, place, at.first):
                    if what == "wo":
                        project_out(which, at, ahead)
                    elif what == "mod":
                        modulation(which, at)
                    else:
                        project((what, which), at, ahead)

            def front(h, at):
                hb, ahead = before(h, at)
                scores(h, 0, at)
                scores(h, 1, at)
                fill(h, 1, at)
                scores(h, 2, at)
                if h or not at.first:
                    transposes(hb, 7, at, ahead)
                scores(h, 3, at)
                if h or not at.first:
                    weighted(hb, 1, at, ahead)
                if h == 0:
                    value_transposes(0, at)
                    value_transposes(1, at)

            def back(h, at):
                scores(h, 4, at)
                fill(h, 2, at)
                transposes(h, 0, at)
                transposes(h, 1, at)
                scores(h, 5, at)
                fill(h, 3, at)
                transposes(h, 2, at)
                transposes(h, 3, at)
                fill(h, 4, at)
                transposes(h, 4, at)
                scores(h, 6, at)
                weighted(h, 0, at)
                transposes(h, 5, at)
                scores(h, 7, at)
                fill(h, 5, at)
                transposes(h, 6, at)

            g0 = Group(0)
            pe.wait_ge(silu_done, 1)
            for k in range(KC):
                pe.wait_ge(mod_in[k], 16)
                for n, m in enumerate(("sa", "ca")):
                    mm = nc.tensor.matmul(ACC[0:1, N.slot("a", ("mod", m), g0), :], silu[:, 3, k:k + 1],
                                          mod_w[:, k, n * D:(n + 1) * D], start=(k == 0), stop=(k == KC - 1))
                    if k == KC - 1:
                        mm.then_inc(a_full, 1)
            pe.wait_ge(ident_in, 16)
            for half in range(2):
                for k in range(KC):
                    if k == 0:
                        pe.wait_ge(xn_done, 4 * (half + 1))
                    if half:
                        pe.wait_ge(h_done, k + 1)
                    for t in range(4):
                        mm = nc.tensor.transpose(S[:, k, t * P:(t + 1) * P],
                                                 x_tile(4 * half + t)[:, k * P:(k + 1) * P], ident[:])
                    mm.then_inc(xt_full, 1)
                    if half == 0 and k == 1:
                        modulation("first", g0)
            pe.wait_ge(h_done, KC)
            project(("k", 0), g0)
            project(("q", (0, 0)), g0)
            pe.wait_ge(h_done, 2 * KC)
            project(("q", (0, 1)), g0)
            project(("k", 1), g0)
            project(("v", 0), g0)
            project(("v", 1), g0)

            for h in range(R - 1):
                front(h, g0)
                back(h, g0)
            front(R - 1, g0)
            with pe.Fori(0, GROUPS - 1) as turn:
                at = Group(1, turn)
                back(R - 1, Group(0, turn))
                for h in range(R - 1):
                    front(h, at)
                    back(h, at)
                front(R - 1, at)

            def weight_bank(name):
                bank_free(name, G7, 0)
                return ACC[:, N.slot("a", name, G7), :]

            def weight_transposes(k):
                bank = weight_bank(("W", k))
                for o in range(KC):
                    mm = nc.tensor.transpose(bank[:, o * P:(o + 1) * P], fw_in[:, o, k * P:(k + 1) * P], ident[:])
                mm.then_inc(a_full, 1)

            scores(3, 4, G7)
            transposes(3, 0, G7)
            transposes(3, 1, G7)
            scores(3, 5, G7)
            pe.wait_ge(f_in, 16)
            weight_transposes(0)
            transposes(3, 2, G7)
            transposes(3, 3, G7)
            weight_transposes(1)
            weighted(3, 0, G7)
            transposes(3, 4, G7)
            scores(3, 6, G7)
            weight_transposes(2)
            transposes(3, 5, G7)
            weight_transposes(3)
            scores(3, 7, G7)
            pe.wait_ge(f_low_in, 16 * 3)
            bank = weight_bank(("A", 0))
            for k in range(KC):
                mm = nc.tensor.transpose(bank[:, k * AG:(k + 1) * AG], ag_in[:, k * P:(k + 1) * P], ident[0:AG, 0:AG])
            mm.then_inc(a_full, 1)
            project_out(0, G7, 0)
            bank = weight_bank(("B", 0))
            for o in range(KC):
                mm = nc.tensor.transpose(bank[0:MAX_R, o * P:(o + 1) * P], fb_in[:, o, :], ident[:])
            mm.then_inc(a_full, 1)
            transposes(3, 6, G7)
            project_out(1, G7, 0)
            transposes(3, 7, G7)
            project_out(2, G7, 0)

            def spread(t):
                s = t % 2
                pe.wait_ge(f_xn, t + 1)
                if t == 0:
                    pe.wait_ge(s_masked, N.value("s", (3, 7), G7))
                if t >= 2:
                    pe.wait_ge(f_aff, t - 1)
                for k in range(KC):
                    mm = nc.tensor.transpose(S[:, 2 + s, k * P:(k + 1) * P], xn2(s)[:, k * P:(k + 1) * P], ident[:])
                mm.then_inc(f_tr, 1)

            def gates(t):
                s = t % 2
                pe.wait_ge(f_aff, t + 1)
                if t == 0:
                    pe.wait_ge(t_lo, N.count["t"])
                if t >= 2:
                    pe.wait_ge(f_tmlo, t - 1)
                for k in range(KC):
                    mm = nc.tensor.matmul(TB[:, s, 0:AG], h2_f(s)[:, k * P:(k + 1) * P], ag_t[:, k, :],
                                          start=(k == 0), stop=(k == KC - 1))
                mm.then_inc(f_gate, 1)

            def kept_ranks(t):
                pe.wait_ge(f_tm, t + 1)
                nc.tensor.transpose(TB[0:MAX_R, t % 2, 2 * P:3 * P], tm(t % 2), ident[:]).then_inc(f_tmt, 1)

            def dense(t):
                s = t % 2
                pe.wait_ge(f_lo, t + 1)
                if t >= 2:
                    pe.wait_ge(f_gated, t - 1)
                n = 0
                for a, b in ((h2_hi(s), fw_hi), (h2_hi(s), fw_lo), (h2_lo(s), fw_hi)):
                    for k in range(KC):
                        mm = nc.tensor.matmul(S[:, s, :], a[:, k, :], b[:, k, :], start=(n == 0), stop=False)
                        n += 1
                mm.then_inc(f_ffn, 1)

            def low_rank(t):
                s = t % 2
                pe.wait_ge(f_tmlo, t + 1)
                for n, (a, b) in enumerate(((tm_hi(s), fb_hi), (tm_hi(s), fb_lo), (tm_lo(s), fb_hi))):
                    mm = nc.tensor.matmul(S[:, s, :], a, b, start=False, stop=(n == 2))
                mm.then_inc(f_full, 1)

            spread(0)
            weighted(3, 1, G7)
            project_out(3, G7, 0)
            for t in range(NT + 1):
                if t + 1 < NT:
                    spread(t + 1)
                if t < NT:
                    gates(t)
                if t >= 1:
                    kept_ranks(t - 1)
                if t < NT:
                    dense(t)
                if t >= 1:
                    low_rank(t - 1)
                if t + 4 < NT:
                    project_out(t + 4, G7, 0)

        @block.scalar
        def _(act):
            def exp(h, i, at):
                need(act, s_masked, N.value("s", (h, i), at))
                nc.scalar.activation(row(i), row(i), ACT.Exp, bias=negmax[:, i:i + 1], scale=-1.0,
                                     accum_out=rowsum[:, i:i + 1]).then_inc(s_exp, 1)

            def transposed_hi(h, i, at, ahead=0):
                for part, js in enumerate(parts(i)):
                    name = (h, i, part)
                    need(act, t_full, N.value("t", name, at, ahead))
                    src = TB[:, N.slot("t", name, at, ahead), 0:len(js) * P].rearrange("p (a b) -> p a b", b=P)
                    nc.scalar.activation(pt_of(i, part, True), src, ACT.Copy).then_inc(t_hi, 1)

            def value_hi(half, at):
                name = ("v", half)
                need(act, t_full, N.value("t", name, at))
                src = TB[:, N.slot("t", name, at), :].rearrange("p (a b) -> p a b", b=P)
                nc.scalar.activation(v_hi[:, 4 * half:4 * half + 4, :], src, ACT.Copy).then_inc(t_hi, 1)

            def output_hi(h, half, at, ahead=0):
                name = (("pva", "pvb")[half], h)
                need(act, a_full, N.value("a", name, at, ahead))
                nc.scalar.activation(o_hi[:, h, half * HALF:(half + 1) * HALF],
                                     ACC[:, N.slot("a", name, at, ahead), :], ACT.Copy).then_inc(a_hi, 1)

            def swap_halves(name, at, ahead=0):
                need(act, a_full, N.value("a", name, at, ahead))
                need(act, r_sum, back_of(N.value("r", name, at, ahead), 2))
                acc = ACC[:, N.slot("a", name, at, ahead), :]
                dst = qr[:, N.slot("r", name, at, ahead), :]
                nc.scalar.activation(dst[0:HD // 2, :], acc[HD // 2:HD, :], ACT.Copy)
                nc.scalar.activation(dst[HD // 2:HD, :], acc[0:HD // 2, :], ACT.Copy).then_inc(a_swapped, 1)

            def rotated_hi(name, at, ahead=0):
                kind, which = name
                need(act, r_sum, N.value("r", name, at, ahead))
                if kind == "k" and which == 0:
                    need(act, s_full, N.value("s", (R - 1, 7), at, ahead - 1))
                dst, half = (q_hi, which[1]) if kind == "q" else (k_hi, which)
                nc.scalar.activation(dst[:, half * HALF:(half + 1) * HALF], qc[:, N.slot("r", name, at, ahead), :],
                                     ACT.Copy).then_inc(r_hi, 1)

            def split_hi(what, at, ahead=0):
                kind, r = what
                s = w_slot(what, at, ahead)
                if kind == "wo":
                    n = (at.g + ahead) * R + r + 1
                    act.wait_ge(wo_scaled, n if at.turn is None else n + at.turn * R)
                else:
                    act.wait_ge(stage_in[s], stage_count(what, at, ahead))
                if kind == "wo":
                    last_use = (("wo", NT - 1), ahead - 1)
                else:
                    last_use = (("q", (r - 1 if r else R - 1, 1)), ahead if r else ahead - 1)
                need(act, a_full, N.value("a", last_use[0], at, last_use[1]))
                dst = {"q": wq_hi, "k": wk_hi, "v": wv_hi}.get(kind)
                dst = wo_hi[:, r, :] if kind == "wo" else dst[:].rearrange("p k n -> p (k n)")
                nc.scalar.activation(dst, stage[:, s, :], ACT.Copy).then_inc(w_hi, 1)

            def fill(h, place, at, jobs=slice(None)):
                for what, which, ahead in fillers(h, place, at.first)[jobs]:
                    if what in "qk":
                        swap_halves((what, which), at, ahead)

            def front(h, at):
                hb, ahead = before(h, at)
                fill(h, 1, at)
                if h or not at.first:
                    transposed_hi(hb, 7, at, ahead)
                exp(h, 0, at)
                exp(h, 1, at)
                exp(h, 2, at)
                if h or not at.first:
                    rotated_hi(("q", (h, 1)), at)
                exp(h, 3, at)
                if h == 0 and not at.first:
                    rotated_hi(("k", 1), at)
                if h < R - 1:
                    split_hi(("q", h + 1), at)
                else:
                    split_hi(("wo", 3), at)
                if h or not at.first:
                    output_hi(hb, 1, at, ahead)
                if h == 0:
                    value_hi(0, at)
                    value_hi(1, at)

            def back(h, at):
                last = h == R - 1
                transposed_hi(h, 0, at)
                transposed_hi(h, 1, at)
                if last:
                    split_hi(("q", 0), at, 1)
                exp(h, 4, at)
                transposed_hi(h, 2, at)
                transposed_hi(h, 3, at)
                exp(h, 5, at)
                if h == 1:
                    split_hi(("wo", 0), at)
                if h == 2:
                    split_hi(("wo", 1), at)
                fill(h, 4, at)
                transposed_hi(h, 4, at)
                if last:
                    split_hi(("k", 0), at, 1)
                output_hi(h, 0, at)
                exp(h, 6, at)
                transposed_hi(h, 5, at)
                rotated_hi(("q", ((h + 1) % R, 0)), at, int(last))
                if h == 2:
                    split_hi(("wo", 2), at)
                exp(h, 7, at)
                fill(h, 5, at, slice(0, 1) if last else slice(0, -1))
                if last:
                    split_hi(("v", 0), at, 1)
                    fill(h, 5, at, slice(1, -1))
                if last:
                    rotated_hi(("k", 0), at, 1)
                transposed_hi(h, 6, at)
                fill(h, 5, at, slice(-1, None))

            g0 = Group(0)
            act.wait_ge(c_in, 16)
            nc.scalar.activation(silu[:, 1, :], silu[:, 0, :], ACT.Exp, scale=-1.0).then_inc(silu_done_exp, 1)
            for t in range(NT):
                act.wait_ge(ln_stat, t + 1)
                nc.scalar.activation(x_tile(t), x_tile(t), ACT.Identity, bias=shift[:, t:t + 1],
                                     scale=rstd[:, t:t + 1]).then_inc(xn_done, 1)
                if t == 3:
                    for n, m in enumerate(("sa", "ca")):
                        number = N.value("a", ("mod", m), Group(0))
                        act.wait_ge(a_full, number)
                        nc.scalar.activation(vt[0:1, n * D:(n + 1) * D], ACC[0:1, N.slot("a", ("mod", m), Group(0)), :],
                                             ACT.Copy).then_inc(a_taken, 1)
            act.wait_ge(a_taken, N.value("a", ("mod", "first"), g0))

            def h_high(n):
                half, k = divmod(n, KC)
                act.wait_ge(h_f32, n + 1)
                nc.scalar.activation(h_hi[:, k, half * HALF:(half + 1) * HALF], S[:, k, :], ACT.Copy).then_inc(h_hi_done, 1)

            for n in range(2 * KC):
                k = n % KC
                act.wait_ge(xt_full, n + 1)
                nc.scalar.activation(S[:, k, :], S[:, k, :], ACT.Identity, bias=modc[:, 0, k:k + 1],
                                     scale=modc[:, 1, k:k + 1]).then_inc(h_f32, 1)
                if n >= 1:
                    h_high(n - 1)
                if n in (4, 5):
                    split_hi(W_FIRST[n - 4], g0)
            h_high(2 * KC - 1)
            swap_halves(("k", 0), g0)
            swap_halves(("q", (0, 0)), g0)
            rotated_hi(("k", 0), g0)
            split_hi(W_FIRST[2], g0)
            swap_halves(("q", (0, 1)), g0)
            rotated_hi(("q", (0, 0)), g0)
            swap_halves(("k", 1), g0)
            rotated_hi(("q", (0, 1)), g0)
            rotated_hi(("k", 1), g0)
            for h in range(R - 1):
                front(h, g0)
                back(h, g0)
            front(R - 1, g0)
            with act.Fori(0, GROUPS - 1) as turn:
                at = Group(1, turn)
                back(R - 1, Group(0, turn))
                for h in range(R - 1):
                    front(h, at)
                    back(h, at)
                front(R - 1, at)

            def weight_hi(name, dst, rows=P, cols=D):
                act.wait_ge(a_full, N.value("a", name, G7))
                nc.scalar.activation(dst, ACC[0:rows, N.slot("a", name, G7), 0:cols], ACT.Copy).then_inc(f_whi, 1)

            transposed_hi(3, 0, G7)
            transposed_hi(3, 1, G7)
            weight_hi(("W", 0), fw_hi[:, 0, :])
            transposed_hi(3, 2, G7)
            transposed_hi(3, 3, G7)
            exp(3, 4, G7)
            weight_hi(("W", 1), fw_hi[:, 1, :])
            exp(3, 5, G7)
            output_hi(3, 0, G7)
            transposed_hi(3, 4, G7)
            weight_hi(("W", 2), fw_hi[:, 2, :])
            transposed_hi(3, 5, G7)
            exp(3, 6, G7)
            weight_hi(("W", 3), fw_hi[:, 3, :])
            weight_hi(("A", 0), vt[:, 0:KC * AG], cols=KC * AG)
            exp(3, 7, G7)
            weight_hi(("B", 0), fb_hi, MAX_R)
            transposed_hi(3, 6, G7)

            def second_norm(t):
                act.wait_ge(f_stat, t + 1)
                if t >= 2:
                    act.wait_ge(f_tr, t - 1)
                else:
                    act.wait_ge(t_full, N.value("t", (3, 3, 0), G7))
                nc.scalar.activation(xn2(t % 2), y[:, t, :], ACT.Identity, bias=shift[:, t:t + 1],
                                     scale=rstd[:, t:t + 1]).then_inc(f_xn, 1)

            def second_h(t):
                s = t % 2
                act.wait_ge(f_tr, t + 1)
                if t >= 2:
                    act.wait_ge(f_gate, t - 1)
                    act.wait_ge(f_lo, t - 1)
                for k in range(KC):
                    ins = nc.scalar.activation(h2_f(s)[:, k * P:(k + 1) * P], S[:, 2 + s, k * P:(k + 1) * P],
                                               ACT.Identity, bias=modc[:, 2, k:k + 1], scale=modc[:, 3, k:k + 1])
                ins.then_inc(f_aff, 1)

            def second_h_hi(t):
                s = t % 2
                act.wait_ge(f_aff, t + 1)
                if t >= 2:
                    act.wait_ge(f_ffn, t - 1)
                nc.scalar.activation(h2_hi(s).rearrange("p k n -> p (k n)"), h2_f(s), ACT.Copy).then_inc(f_hi, 1)

            def router_exp(t):
                s = t % 2
                act.wait_ge(f_smax, t + 1)
                nc.scalar.activation(gs[:, s, 1, :], gs[:, s, 0, :], ACT.Exp, bias=gs[:, s, 2, 0:1], scale=-1.0,
                                     accum_out=gs[:, s, 2, 1:2]).then_inc(f_exp, 1)

            transposed_hi(3, 7, G7)
            second_norm(0)
            second_norm(1)
            second_h(0)
            second_h_hi(0)
            output_hi(3, 1, G7)
            for t in range(NT + 1):
                if t + 1 < NT:
                    second_h(t + 1)
                if t < NT:
                    router_exp(t)
                if t >= 1:
                    s = (t - 1) % 2
                    act.wait_ge(f_tmt, t)
                    nc.scalar.activation(tm_hi(s), TB[0:MAX_R, s, 2 * P:3 * P], ACT.Copy).then_inc(f_tmhi, 1)
                if t + 1 < NT:
                    second_h_hi(t + 1)
                if t + 2 < NT:
                    second_norm(t + 2)

        @block.vector
        def _(dve):
            linked = [0]

            def link(ins):
                linked[0] += 1
                ins.then_inc(vec, 1)
                dve.wait_ge(vec, linked[0])

            def masked(h, i, at):
                hb, ahead = before(h, at)
                if i < 6:
                    old = i if i < 4 else i + 2
                    row_free = N.value("t", (hb, old, len(parts(old)) - 1), at, ahead)
                else:
                    row_free = N.value("t", (h, i - 2, 1), at)
                need_apart(dve, dve_passed, (s_full, N.value("s", (h, i), at)), (t_full, row_free))
                n, c0 = P * (i + 1), score_at(i)
                nc.vector.tensor_tensor_reduce(row(i), S_flat[:, c0:c0 + n], mask[:, T - n:T], -SCALE, 3.4e38,
                                               ALU.add, ALU.min, negmax[:, i:i + 1]).then_inc(s_masked, 1)

            def inverse(h, i, at):
                need(dve, s_exp, N.value("s", (h, i), at))
                nc.vector.reciprocal(rowinv[:, i:i + 1], rowsum[:, i:i + 1]).then_inc(s_inv, 1)

            def transposed_lo(h, i, at, ahead=0):
                for part, js in enumerate(parts(i)):
                    name = (h, i, part)
                    need(dve, t_hi, N.value("t", name, at, ahead))
                    src = TB[:, N.slot("t", name, at, ahead), 0:len(js) * P].rearrange("p (a b) -> p a b", b=P)
                    nc.vector.tensor_tensor(pt_of(i, part, False), src, f32(pt_of(i, part, True)),
                                            ALU.subtract).then_inc(t_lo, 1)

            def value_lo(half, at):
                name = ("v", half)
                need(dve, t_hi, N.value("t", name, at))
                src = TB[:, N.slot("t", name, at), :].rearrange("p (a b) -> p a b", b=P)
                rows = slice(4 * half, 4 * half + 4)
                nc.vector.tensor_tensor(v_lo[:, rows, :], src, f32(v_hi[:, rows, :]), ALU.subtract).then_inc(t_lo, 1)

            def output_lo(h, half, at, ahead=0):
                name = (("pva", "pvb")[half], h)
                n = 2 * h + half + 1
                n = n + 2 * R * (at.g + ahead) if at.turn is None else n + 2 * R * (at.g + ahead) + at.turn * (2 * R)
                dve.wait_ge(a_hi, n)
                cols = slice(half * HALF, (half + 1) * HALF)
                nc.vector.tensor_tensor(o_lo[:, h, cols], ACC[:, N.slot("a", name, at, ahead), :],
                                        f32(o_hi[:, h, cols]), ALU.subtract).then_inc(a_taken, 1)

            def times_cos(name, at, ahead=0):
                kind, which = name
                half = which[1] if kind == "q" else which
                need(dve, a_swapped, N.value("r", name, at, ahead))
                need(dve, r_lo, back_of(N.value("r", name, at, ahead), 2))
                nc.vector.tensor_tensor(qc[:, N.slot("r", name, at, ahead), :], ACC[:, N.slot("a", name, at, ahead), :],
                                        trig[:, 0, half * HALF:(half + 1) * HALF], ALU.mult).then_inc(a_taken, 1)

            def rotated_lo(name, at, ahead=0):
                kind, which = name
                half = which[1] if kind == "q" else which
                cols = slice(half * HALF, (half + 1) * HALF)
                hi, lo = (q_hi, q_lo) if kind == "q" else (k_hi, k_lo)
                need(dve, r_hi, N.value("r", name, at, ahead))
                nc.vector.tensor_tensor(lo[:, cols], qc[:, N.slot("r", name, at, ahead), :], f32(hi[:, cols]),
                                        ALU.subtract).then_inc(r_lo, 1)

            def copy_values(half, at, ahead=0):
                name = ("v", half)
                need(dve, a_full, N.value("a", name, at, ahead))
                need(dve, t_full, N.value("t", name, at, ahead - 1))
                nc.vector.tensor_copy(vt[:, half * HALF:(half + 1) * HALF],
                                      ACC[:, N.slot("a", name, at, ahead), :]).then_inc(a_taken, 1)

            def add_output(t, at, ahead):
                name = ("wo", t)
                need(dve, a_full, N.value("a", name, at, ahead))
                dve.wait_ge(y_in, 16)
                need(dve, a_taken, back_of(N.value("a", name, at, ahead), 2))
                nc.vector.tensor_tensor(y[:, t, :], ACC[:, N.slot("a", name, at, ahead), :], y[:, t, :],
                                        ALU.add).then_inc(a_taken, 1)

            def split_lo(what, at, ahead=0):
                kind, r = what
                s = w_slot(what, at, ahead)
                dve.wait_ge(w_hi, w_number(what, at, ahead))
                hi, lo = {"q": (wq_hi, wq_lo), "k": (wk_hi, wk_lo), "v": (wv_hi, wv_lo), "wo": (wo_hi, wo_lo)}[kind]
                if kind == "wo":
                    hi, lo = hi[:, r, :], lo[:, r, :]
                else:
                    hi, lo = hi[:].rearrange("p k n -> p (k n)"), lo[:].rearrange("p k n -> p (k n)")
                nc.vector.tensor_tensor(lo, stage[:, s, :], f32(hi), ALU.subtract).then_inc(w_lo, 1)

            def take_modulation(m, at):
                name = ("mod", m)
                dve.wait_ge(a_full, N.value("a", name, at))
                acc = ACC[:, N.slot("a", name, at), :]
                if m in ("sb", "cb"):
                    dve.wait_ge(t_full, N.value("t", ("v", 1), at))
                    c0 = 0 if m == "sb" else D
                    nc.vector.tensor_copy(vt[0:1, c0:c0 + D], acc[0:1, :]).then_inc(a_taken, 1)
                elif m in ("first", "second"):
                    r = 0 if m == "first" else 2
                    nc.vector.tensor_copy(modc[:, r, :], acc[:, 0:KC])
                    nc.vector.tensor_scalar(modc[:, r + 1, :], acc[:, KC:2 * KC], 1.0, None, ALU.add).then_inc(a_taken, 1)
                else:
                    gate = ga_b if m == "ga" else gb_b
                    link(nc.vector.tensor_scalar(gate[:], acc, 0.0, 2.0, ALU.is_ge, ALU.mult))
                    link(nc.vector.scalar_tensor_tensor(out=acc, in0=gate[:], scalar=-1.0, in1=acc, op0=ALU.add,
                                                        op1=ALU.mult))
                    link(nc.vector.tensor_scalar(acc, acc, 0.25, None, ALU.max))
                    nc.vector.scalar_tensor_tensor(out=gate[:], in0=gate[:], scalar=-1.0, in1=acc, op0=ALU.add,
                                                   op1=ALU.mult).then_inc(a_taken, 1)

            def fill(h, place, at, jobs=slice(None), back=0):
                for what, which, ahead in fillers(h, place, at.g == back)[jobs]:
                    ahead -= back
                    if what in "qk":
                        times_cos((what, which), at, ahead)
                    elif what == "v":
                        copy_values(which, at, ahead)
                    elif what == "wo":
                        add_output(which, at, ahead)
                    else:
                        take_modulation(which, at)
                        if which == "second":
                            dve.wait_ge(tab_in, 32)
                            for k in range(KC):
                                ins = nc.vector.tensor_scalar(vt[:, k * P:(k + 1) * P], mask[:, 0:P],
                                                              silu[:, 3, k:k + 1], None, ALU.add)
                            ins.then_inc(silu_done, 1)

            def front(h, at):
                hb, ahead = before(h, at)
                masked(h, 0, at)
                masked(h, 1, at)
                if h or not at.first:
                    fill(hb, 5, at, slice(-1, None), -ahead)
                fill(h, 1, at)
                masked(h, 2, at)
                if h or not at.first:
                    transposed_lo(hb, 7, at, ahead)
                masked(h, 3, at)
                for i in range(3):
                    inverse(h, i, at)
                if h or not at.first:
                    rotated_lo(("q", (h, 1)), at)
                inverse(h, 3, at)
                if h == 0 and not at.first:
                    rotated_lo(("k", 1), at)
                if h < R - 1:
                    split_lo(("q", h + 1), at)
                else:
                    split_lo(("wo", 3), at)
                if h or not at.first:
                    output_lo(hb, 1, at, ahead)
                if h == 0:
                    value_lo(0, at)
                    value_lo(1, at)

            def back(h, at):
                last = h == R - 1
                if h == 0:
                    masked(h, 4, at)
                fill(h, 2, at)
                transposed_lo(h, 0, at)
                transposed_lo(h, 1, at)
                if last:
                    split_lo(("q", 0), at, 1)
                if h:
                    masked(h, 4, at)
                masked(h, 5, at)
                inverse(h, 4, at)
                fill(h, 3, at)
                transposed_lo(h, 2, at)
                transposed_lo(h, 3, at)
                inverse(h, 5, at)
                if h == 1:
                    split_lo(("wo", 0), at)
                if h == 2:
                    split_lo(("wo", 1), at)
                fill(h, 4, at, slice(0, -1))
                transposed_lo(h, 4, at)
                masked(h, 6, at)
                fill(h, 4, at, slice(-1, None))
                if last:
                    split_lo(("k", 0), at, 1)
                output_lo(h, 0, at)
                inverse(h, 6, at)
                masked(h, 7, at)
                transposed_lo(h, 5, at)
                rotated_lo(("q", ((h + 1) % R, 0)), at, int(last))
                inverse(h, 7, at)
                if h == 2:
                    split_lo(("wo", 2), at)
                fill(h, 5, at, slice(0, 1) if last else slice(0, -1))
                if last:
                    split_lo(("v", 0), at, 1)
                    fill(h, 5, at, slice(1, -1))
                if last:
                    rotated_lo(("k", 0), at, 1)
                transposed_lo(h, 6, at)

            def norm(x_t, t, done):
                link(nc.vector.bn_stats(stats[:, t, :], x_t))
                link(nc.vector.bn_aggr(mv[:, t, :], stats[:, t, :]))
                nc.vector.tensor_scalar(rstd[:, t:t + 1], mv[:, t, 1:2], EPS, None, ALU.add).then_inc(done, 1)

            dve.wait_ge(silu_done_exp, 1)
            link(nc.vector.tensor_scalar(silu[:, 1, :], silu[:, 1, :], 1.0, None, ALU.add))
            link(nc.vector.reciprocal(silu[:, 2, :], silu[:, 1, :]))
            nc.vector.tensor_tensor(silu[:, 3, :], silu[:, 0, :], silu[:, 2, :], ALU.mult).then_inc(silu_done, 1)
            for t in range(NT):
                dve.wait_ge(x_in[t], 16)
                norm(x_tile(t), t, ln_var)
            g0 = Group(0)
            take_modulation("first", g0)
            for n in range(2 * KC):
                half, k = divmod(n, KC)
                cols = slice(half * HALF, (half + 1) * HALF)
                dve.wait_ge(h_hi_done, n + 1)
                nc.vector.tensor_tensor(h_lo[:, k, cols], S[:, k, :],
                                        f32(h_hi[:, k, cols]), ALU.subtract).then_inc(h_done, 1)
                if n in (3, 4):
                    split_lo(W_FIRST[n - 3], g0)
            dve.wait_ge(tab_in, 32)
            times_cos(("k", 0), g0)
            times_cos(("q", (0, 0)), g0)
            rotated_lo(("k", 0), g0)
            split_lo(W_FIRST[2], g0)
            times_cos(("q", (0, 1)), g0)
            rotated_lo(("q", (0, 0)), g0)
            times_cos(("k", 1), g0)
            rotated_lo(("q", (0, 1)), g0)
            rotated_lo(("k", 1), g0)
            copy_values(0, g0)
            copy_values(1, g0)
            for h in range(R - 1):
                front(h, g0)
                back(h, g0)
            front(R - 1, g0)
            with dve.Fori(0, GROUPS - 1) as turn:
                at = Group(1, turn)
                back(R - 1, Group(0, turn))
                for h in range(R - 1):
                    front(h, at)
                    back(h, at)
                front(R - 1, at)

            def weight_lo(name, number, hi=None, lo=None, rows=P):
                dve.wait_ge(f_whi, number)
                if hi is None:
                    nc.vector.engine_nop().then_inc(a_taken, 1)
                else:
                    nc.vector.tensor_tensor(lo, ACC[0:rows, N.slot("a", name, G7), :], f32(hi), ALU.subtract).then_inc(a_taken, 1)

            transposed_lo(3, 0, G7)
            transposed_lo(3, 1, G7)
            masked(3, 4, G7)
            weight_lo(("W", 0), 1, fw_hi[:, 0, :], fw_lo[:, 0, :])
            transposed_lo(3, 2, G7)
            transposed_lo(3, 3, G7)
            inverse(3, 4, G7)
            masked(3, 5, G7)
            weight_lo(("W", 1), 2, fw_hi[:, 1, :], fw_lo[:, 1, :])
            inverse(3, 5, G7)
            output_lo(3, 0, G7)
            transposed_lo(3, 4, G7)
            masked(3, 6, G7)
            weight_lo(("W", 2), 3, fw_hi[:, 2, :], fw_lo[:, 2, :])
            transposed_lo(3, 5, G7)
            inverse(3, 6, G7)
            weight_lo(("W", 3), 4, fw_hi[:, 3, :], fw_lo[:, 3, :])
            masked(3, 7, G7)
            weight_lo(("A", 0), 5)
            inverse(3, 7, G7)
            add_output(0, G7, 0)
            weight_lo(("B", 0), 6, fb_hi, fb_lo, MAX_R)
            transposed_lo(3, 6, G7)
            add_output(1, G7, 0)

            def second_norm(t):
                dve.wait_ge(a_taken, N.value("a", ("wo", t), G7))
                norm(y[:, t, :], t, f_var)

            second_norm(0)
            transposed_lo(3, 7, G7)
            second_norm(1)
            add_output(2, G7, 0)

            def second_h_lo(t):
                s = t % 2
                dve.wait_ge(f_hi, t + 1)
                nc.vector.tensor_tensor(h2_lo(s).rearrange("p k n -> p (k n)"), h2_f(s),
                                        f32(h2_hi(s).rearrange("p k n -> p (k n)")), ALU.subtract).then_inc(f_lo, 1)

            def router_logits(t):
                s = t % 2
                dve.wait_ge(f_gate, t + 1)
                if t == 0:
                    dve.wait_ge(b_in, 32)
                nc.vector.tensor_tensor_reduce(gs[:, s, 0, :], TB[:, s, MAX_R:AG], gate_bb[:], -1.0, 3.4e38, ALU.add,
                                               ALU.min, gs[:, s, 2, 0:1]).then_inc(f_smax, 1)

            def route(t):
                s = t % 2
                e, prob, worse, keyed = (gs[:, s, n, :] for n in (1, 3, 4, 5))
                total, inv_total, top, inv_top = gs[:, s, 2, 1:2], gs[:, s, 2, 2:3], gs[:, s, 6, 0:1], gs[:, s, 6, 1:2]
                rank = gs[:, s, 6, 2:3]
                dve.wait_ge(f_exp, t + 1)
                link(nc.vector.reciprocal(inv_total, total))
                link(nc.vector.tensor_scalar(prob, e, inv_total, None, ALU.mult))
                link(nc.vector.reduce_max(top, prob, AX_X))
                link(nc.vector.tensor_scalar(worse, prob, top, 2.0 * MAX_R, ALU.is_lt, ALU.mult))
                nc.vector.reciprocal(inv_top, top)
                link(nc.vector.tensor_tensor_reduce(keyed, worse, ranks[:, 0:NR], 1.0, 3.4e38, ALU.add, ALU.min, rank))
                link(nc.vector.tensor_scalar(tm_f(s), TB[:, s, 0:MAX_R], top, inv_top, ALU.mult, ALU.mult))
                nc.vector.scalar_tensor_tensor(out=tm(s), in0=ranks[:, NR:NR + MAX_R], scalar=rank, in1=tm_f(s), op0=ALU.is_lt,
                                               op1=ALU.mult).then_inc(f_tm, 1)

            def kept_ranks_lo(t):
                s = t % 2
                dve.wait_ge(f_tmhi, t + 1)
                nc.vector.tensor_tensor(tm_lo(s), TB[0:MAX_R, s, 2 * P:3 * P], f32(tm_hi(s)), ALU.subtract).then_inc(f_tmlo, 1)

            def gated(t):
                dve.wait_ge(f_full, t + 1)
                if t >= 2:
                    dve.wait_ge(f_out, t - 1)
                nc.vector.tensor_tensor(f_tmp(t % 2), S[:, t % 2, :], gb_b[:], ALU.mult).then_inc(f_gated, 1)

            second_h_lo(0)
            output_lo(3, 1, G7)
            add_output(3, G7, 0)
            for t in range(NT + 1):
                if t < NT:
                    router_logits(t)
                if t + 2 < NT:
                    second_norm(t + 2)
                if t >= 1:
                    kept_ranks_lo(t - 1)
                if t < NT:
                    route(t)
                if t + 1 < NT:
                    second_h_lo(t + 1)
                if t >= 1:
                    gated(t - 1)
                if t + 4 < NT:
                    add_output(t + 4, G7, 0)

        @block.gpsimd
        def _(pool):
            def normalise(h, i, at):
                need_apart(pool, pool_passed, (s_inv, N.value("s", (h, i), at)))
                nc.gpsimd.tensor_scalar(row(i), row(i), rowinv[:, i:i + 1], 1.0, ALU.mult, ALU.mult).then_inc(s_norm, 1)

            def rotate(name, at, ahead=0):
                kind, which = name
                half = which[1] if kind == "q" else which
                s = N.slot("r", name, at, ahead)
                n = N.value("r", name, at, ahead)
                need(pool, a_swapped, n)
                nc.gpsimd.tensor_tensor(qr[:, s, :], qr[:, s, :], trig[:, 1, half * HALF:(half + 1) * HALF],
                                        ALU.mult).then_inc(r_sin, 1)
                need(pool, r_sin, n)
                need(pool, a_taken, N.value("a", name, at, ahead))
                nc.gpsimd.tensor_tensor(qc[:, s, :], qc[:, s, :], qr[:, s, :], ALU.add).then_inc(r_sum, 1)

            def scale_wo(r, at):
                s = w_slot(("wo", r), at)
                pool.wait_ge(stage_in[s], stage_count(("wo", r), at))
                nc.gpsimd.tensor_tensor(stage[:, s, :], stage[:, s, :], ga_b[:], ALU.mult).then_inc(wo_scaled, 1)

            def front(h, at):
                if h or not at.first:
                    rotate(("q", (h, 1)), at)
                if h == 0 and not at.first:
                    rotate(("k", 1), at)
                if h == R - 1:
                    scale_wo(3, at)
                normalise(h, 0, at)
                normalise(h, 1, at)
                normalise(h, 2, at)
                normalise(h, 3, at)

            def back(h, at):
                last = h == R - 1
                if h in (1, 2):
                    scale_wo(h - 1, at)
                normalise(h, 4, at)
                normalise(h, 5, at)
                if h == 2:
                    scale_wo(2, at)
                rotate(("q", ((h + 1) % R, 0)), at, int(last))
                normalise(h, 6, at)
                normalise(h, 7, at)
                if last:
                    rotate(("k", 0), at, 1)

            for buf, tile in ((pa_hi, 11), (pa_lo, 11), (pb_hi, 27), (pb_lo, 27)):
                nc.gpsimd.memset(f32(buf[:, tile, :]), 0.0)
            g0 = Group(0)
            roots = [0]

            def root_and_shift(t, var, done):
                pool.wait_ge(var, t + 1)
                nc.gpsimd.tensor_tensor(rstd[:, t:t + 1], rstd[:, t:t + 1], ranks[:, NR + MAX_R:], ALU.pow).then_inc(root, 1)
                roots[0] += 1
                pool.wait_ge(root, roots[0])
                nc.gpsimd.tensor_scalar(shift[:, t:t + 1], mv[:, t, 0:1], rstd[:, t:t + 1], -1.0, ALU.mult,
                                        ALU.mult).then_inc(done, 1)

            pool.wait_ge(ranks_in, 16)
            for t in range(NT):
                root_and_shift(t, ln_var, ln_stat)
            pool.wait_ge(tab_in, 32)
            rotate(("k", 0), g0)
            rotate(("q", (0, 0)), g0)
            rotate(("q", (0, 1)), g0)
            rotate(("k", 1), g0)
            for h in range(R - 1):
                front(h, g0)
                if h == 1:
                    pool.wait_ge(a_taken, N.value("a", ("mod", "ga"), g0))
                back(h, g0)
            front(R - 1, g0)
            with pool.Fori(0, GROUPS - 1) as turn:
                at = Group(1, turn)
                back(R - 1, Group(0, turn))
                for h in range(R - 1):
                    front(h, at)
                    back(h, at)
                front(R - 1, at)
            for i in range(4, 8):
                normalise(3, i, G7)
            root_and_shift(0, f_var, f_stat)
            root_and_shift(1, f_var, f_stat)
            pool.wait_ge(b_in, 32)
            nc.gpsimd.tensor_tensor(ffn_bias, ffn_bias, gb_b[:], ALU.mult).then_inc(f_bias, 1)
            pool.wait_ge(f_bias, 1)

            def add_bias(t):
                pool.wait_ge(f_xn, t + 1)
                nc.gpsimd.tensor_tensor(y[:, t, :], y[:, t, :], ffn_bias, ALU.add).then_inc(f_y, 1)

            add_bias(0)
            for t in range(NT + 1):
                if t + 2 < NT:
                    root_and_shift(t + 2, f_var, f_stat)
                if t + 1 < NT:
                    add_bias(t + 1)
                if t >= 1:
                    pool.wait_ge(f_y, t)
                    pool.wait_ge(f_gated, t)
                    nc.gpsimd.tensor_tensor(y[:, t - 1, :], y[:, t - 1, :], f_tmp((t - 1) % 2), ALU.add).then_inc(f_out, 1)
    return nc


_INS = ["L0_attn_x", "L0_attn_wq", "L0_attn_wk", "L0_attn_wv", "L0_attn_wo", "L0_ffn_W", "L0_ffn_b", "L0_ffn_A",
        "L0_ffn_B", "L0_ffn_gate_w", "L0_ffn_gate_b", "L0_c", "L0_wmod"]
_OUTS = [((1, T, D), "float32")]


def kernel(**inputs):
    import numpy as _np
    import concourse.bacc as _bacc
    from concourse import mybir as _mybir
    from concourse.bass_utils import run_bass_kernel_spmd as _run

    nc = _bacc.Bacc("TRN2", target_bir_lowering=False, num_devices=1, dynamic_dma_scratch_size=1024)
    arrays, args = {}, []
    for name in _INS:
        a = _np.ascontiguousarray(inputs[name])
        arrays[f"in_{name}_dram"] = a
        args.append(nc.dram_tensor(f"in_{name}_dram", a.shape, _mybir.dt.from_np(a.dtype), kind="ExternalInput").ap())
    for i, (shape, dtype) in enumerate(_OUTS):
        dt = _mybir.dt.from_np(_np.dtype(dtype))
        args.append(nc.dram_tensor(f"out_{i}_dram", shape, dt, kind="ExternalOutput").ap())
    adaln_block(nc, *args)
    r = _run(nc, [arrays], core_ids=[0])
    got = tuple(r.results[0][f"out_{i}_dram"] for i in range(len(_OUTS)))
    return got[0]
```
